# Optimizing a Trainium2 kernel written in Bass

```python
import numpy as np
import jax
import jax.numpy as jnp

def _softmax(x, axis=-1):
    return jax.nn.softmax(x, axis=axis)

def _gelu(x):
    return jax.nn.gelu(x, approximate=True)

def _silu(x):
    return jax.nn.silu(x)

def _sigmoid(x):
    return jax.nn.sigmoid(x)

def _layernorm(x, axis=-1, eps=1e-05):
    m = jnp.mean(x, axis=axis, keepdims=True)
    v = jnp.var(x, axis=axis, keepdims=True)
    return (x - m) / jnp.sqrt(v + eps)

def _scatter_add(tgt, idx, src, axis=0):
    return tgt.at[idx].add(src)

def _segment_sum(src, seg, n):
    return jax.ops.segment_sum(src, seg, n)
kernel_name = 'mk_seq_preln_d1_jaxref_r4_4eb185'

def setup_inputs(seed: int=0):
    np.random.seed(seed)
    _w = jnp.asarray

    def _L0_attn_setup():
        import jax, jax.numpy as jnp
        import numpy as np
        D_MODEL = 256
        D_STATE = 16
        D_CONV = 4
        EXPAND = 2
        D_INNER = EXPAND * D_MODEL
        DT_RANK = D_MODEL // 16
        B_, L_ = (2, 256)

        def _selective_scan(u, dt, A, Bm, Cm, D):
            dA = jnp.exp(dt[..., None] * A)
            dBu = (dt * u)[..., None] * Bm[:, :, None, :]

            def step(h, inp):
                dA_t, dBu_t = inp
                h = dA_t * h + dBu_t
                return (h, h)
            h0 = jnp.zeros((u.shape[0], u.shape[2], A.shape[1]), u.dtype)
            _, hs = jax.lax.scan(step, h0, (dA.swapaxes(0, 1), dBu.swapaxes(0, 1)))
            y = jnp.einsum('lbdn,bln->bld', hs, Cm)
            return y + u * D
        key = jax.random.key(seed)
        ks = jax.random.split(key, 8)
        s = 0.02
        A_log = jnp.log(jnp.tile(jnp.arange(1, D_STATE + 1, dtype=jnp.float32)[None, :], (D_INNER, 1)))
        return {'x': jax.random.normal(ks[0], (B_, L_, D_MODEL), jnp.float32), 'ln_g': jnp.ones((D_MODEL,), jnp.float32), 'ln_b': jnp.zeros((D_MODEL,), jnp.float32), 'in_proj_w': jax.random.normal(ks[1], (2 * D_INNER, D_MODEL), jnp.float32) * s, 'conv_w': jax.random.normal(ks[2], (D_INNER, 1, D_CONV), jnp.float32) * s, 'conv_b': jnp.zeros((D_INNER,), jnp.float32), 'x_proj_w': jax.random.normal(ks[3], (DT_RANK + 2 * D_STATE, D_INNER), jnp.float32) * s, 'dt_proj_w': jax.random.normal(ks[4], (D_INNER, DT_RANK), jnp.float32) * s, 'dt_proj_b': jnp.full((D_INNER,), -4.6, jnp.float32), 'A_log': A_log, 'D': jnp.ones((D_INNER,), jnp.float32), 'out_proj_w': jax.random.normal(ks[5], (D_MODEL, D_INNER), jnp.float32) * s, 'glu_w': jax.random.normal(ks[6], (2 * D_MODEL, D_MODEL), jnp.float32) * s, 'glu_b': jnp.zeros((2 * D_MODEL,), jnp.float32)}
    _L0_attn_in = _L0_attn_setup()

    def _L0_ffn_setup():
        import jax, jax.numpy as jnp
        import numpy as np
        TOP_K = 8
        CAPACITY = 128

        def _silu(x):
            return x * jax.nn.sigmoid(x)
        key = jax.random.key(seed)
        ks = jax.random.split(key, 7)
        B, S, H, E, I, Is = (2, 256, 256, 64, 128, 512)
        s = 0.05
        return {'hidden_states': jax.random.normal(ks[0], (B, S, H), jnp.float32), 'gate_w': jax.random.normal(ks[1], (H, E), jnp.float32) * s, 'shared_gate_w': jax.random.normal(ks[2], (H, 1), jnp.float32) * s, 'shared_gate_up_w': jax.random.normal(ks[3], (H, 2 * Is), jnp.float32) * s, 'shared_down_w': jax.random.normal(ks[4], (Is, H), jnp.float32) * s, 'expert_gate_up_w': jax.random.normal(ks[5], (E, H, 2 * I), jnp.float32) * s, 'expert_down_w': jax.random.normal(ks[6], (E, I, H), jnp.float32) * s}
    _L0_ffn_in = _L0_ffn_setup()
    _d = {'L0_attn_x': _L0_attn_in['x'], 'L0_attn_ln_g': _L0_attn_in['ln_g'], 'L0_attn_ln_b': _L0_attn_in['ln_b'], 'L0_attn_in_proj_w': _L0_attn_in['in_proj_w'], 'L0_attn_conv_w': _L0_attn_in['conv_w'], 'L0_attn_conv_b': _L0_attn_in['conv_b'], 'L0_attn_x_proj_w': _L0_attn_in['x_proj_w'], 'L0_attn_dt_proj_w': _L0_attn_in['dt_proj_w'], 'L0_attn_dt_proj_b': _L0_attn_in['dt_proj_b'], 'L0_attn_A_log': _L0_attn_in['A_log'], 'L0_attn_D': _L0_attn_in['D'], 'L0_attn_out_proj_w': _L0_attn_in['out_proj_w'], 'L0_attn_glu_w': _L0_attn_in['glu_w'], 'L0_attn_glu_b': _L0_attn_in['glu_b'], 'L0_ffn_gate_w': _L0_ffn_in['gate_w'], 'L0_ffn_shared_gate_w': _L0_ffn_in['shared_gate_w'], 'L0_ffn_shared_gate_up_w': _L0_ffn_in['shared_gate_up_w'], 'L0_ffn_shared_down_w': _L0_ffn_in['shared_down_w'], 'L0_ffn_expert_gate_up_w': _L0_ffn_in['expert_gate_up_w'], 'L0_ffn_expert_down_w': _L0_ffn_in['expert_down_w']}
    _x0 = _d['L0_attn_x']
    _d['L0_attn_x'] = jax.random.normal(jax.random.fold_in(jax.random.key(seed), 1), (32, 512, 256), dtype=_x0.dtype)
    del _x0
    return _d

def reference(L0_attn_x, L0_attn_ln_g, L0_attn_ln_b, L0_attn_in_proj_w, L0_attn_conv_w, L0_attn_conv_b, L0_attn_x_proj_w, L0_attn_dt_proj_w, L0_attn_dt_proj_b, L0_attn_A_log, L0_attn_D, L0_attn_out_proj_w, L0_attn_glu_w, L0_attn_glu_b, L0_ffn_gate_w, L0_ffn_shared_gate_w, L0_ffn_shared_gate_up_w, L0_ffn_shared_down_w, L0_ffn_expert_gate_up_w, L0_ffn_expert_down_w):

    def _L0_attn_ref(x, ln_g, ln_b, in_proj_w, conv_w, conv_b, x_proj_w, dt_proj_w, dt_proj_b, A_log, D, out_proj_w, glu_w, glu_b):
        import jax, jax.numpy as jnp
        import numpy as np
        D_MODEL = 256
        D_STATE = 16
        D_CONV = 4
        EXPAND = 2
        D_INNER = EXPAND * D_MODEL
        DT_RANK = D_MODEL // 16
        B_, L_ = (2, 256)

        def _selective_scan(u, dt, A, Bm, Cm, D):
            dA = jnp.exp(dt[..., None] * A)
            dBu = (dt * u)[..., None] * Bm[:, :, None, :]

            def step(h, inp):
                dA_t, dBu_t = inp
                h = dA_t * h + dBu_t
                return (h, h)
            h0 = jnp.zeros((u.shape[0], u.shape[2], A.shape[1]), u.dtype)
            _, hs = jax.lax.scan(step, h0, (dA.swapaxes(0, 1), dBu.swapaxes(0, 1)))
            y = jnp.einsum('lbdn,bln->bld', hs, Cm)
            return y + u * D
        skip = x
        mu = x.mean(-1, keepdims=True)
        var = x.var(-1, keepdims=True)
        xn = (x - mu) * jax.lax.rsqrt(var + 1e-05) * ln_g + ln_b
        xz = xn @ in_proj_w.T
        xp, z = (xz[..., :D_INNER], xz[..., D_INNER:])
        xc = jax.lax.conv_general_dilated(xp.transpose(0, 2, 1), conv_w, (1,), [(D_CONV - 1, 0)], dimension_numbers=('NCH', 'OIH', 'NCH'), feature_group_count=D_INNER)
        xc = jax.nn.silu((xc + conv_b[:, None]).transpose(0, 2, 1))
        x_dbl = xc @ x_proj_w.T
        dt = x_dbl[..., :DT_RANK]
        Bm = x_dbl[..., DT_RANK:DT_RANK + D_STATE]
        Cm = x_dbl[..., DT_RANK + D_STATE:]
        dt = jax.nn.softplus(dt @ dt_proj_w.T + dt_proj_b)
        A = -jnp.exp(A_log)
        y = _selective_scan(xc, dt, A, Bm, Cm, D)
        y = y * jax.nn.silu(z)
        m = y @ out_proj_w.T
        m = jax.nn.gelu(m, approximate=False)
        g = m @ glu_w.T + glu_b
        m = g[..., :D_MODEL] * jax.nn.sigmoid(g[..., D_MODEL:])
        return m + skip

    def _L0_ffn_ref(hidden_states, gate_w, shared_gate_w, shared_gate_up_w, shared_down_w, expert_gate_up_w, expert_down_w):
        import jax, jax.numpy as jnp
        import numpy as np
        TOP_K = 8
        CAPACITY = 128

        def _silu(x):
            return x * jax.nn.sigmoid(x)
        B, S, H = hidden_states.shape
        x = hidden_states.reshape(-1, H)
        T = x.shape[0]
        E = gate_w.shape[1]
        Is = shared_gate_up_w.shape[1] // 2
        I = expert_gate_up_w.shape[2] // 2
        gu = x @ shared_gate_up_w
        shared = _silu(gu[:, :Is]) * gu[:, Is:] @ shared_down_w
        shared = shared * jax.nn.sigmoid(x @ shared_gate_w)
        logits = x @ gate_w
        probs = jax.nn.softmax(logits.astype(jnp.float32), axis=-1)
        w, idx = jax.lax.top_k(probs, TOP_K)
        w = (w / jnp.sum(w, axis=-1, keepdims=True)).astype(x.dtype)
        e_flat = idx.reshape(-1)
        w_flat = w.reshape(-1)
        A = e_flat.shape[0]
        tok = jnp.arange(A) // TOP_K
        onehot = jax.nn.one_hot(e_flat, E, dtype=jnp.int32)
        pos = jnp.take_along_axis(jnp.cumsum(onehot, axis=0) - 1, e_flat[:, None], axis=1)[:, 0]
        slot = jnp.minimum(pos, CAPACITY)
        buf = jnp.zeros((E, CAPACITY + 1, H), x.dtype).at[e_flat, slot].set(x[tok])
        gu_e = jnp.einsum('ech,ehf->ecf', buf, expert_gate_up_w)
        act = _silu(gu_e[..., :I]) * gu_e[..., I:]
        out_e = jnp.einsum('eci,eih->ech', act, expert_down_w)
        y = out_e[e_flat, slot] * w_flat[:, None]
        y = jnp.where((pos < CAPACITY)[:, None], y, jnp.zeros_like(y))
        y = y.reshape(T, TOP_K, H).sum(axis=1)
        return (y + shared).reshape(B, S, H)
    x = L0_attn_x
    x = x + _L0_attn_ref(_layernorm(x, axis=-1), L0_attn_ln_g, L0_attn_ln_b, L0_attn_in_proj_w, L0_attn_conv_w, L0_attn_conv_b, L0_attn_x_proj_w, L0_attn_dt_proj_w, L0_attn_dt_proj_b, L0_attn_A_log, L0_attn_D, L0_attn_out_proj_w, L0_attn_glu_w, L0_attn_glu_b)
    x = x + _L0_ffn_ref(_layernorm(x, axis=-1), L0_ffn_gate_w, L0_ffn_shared_gate_w, L0_ffn_shared_gate_up_w, L0_ffn_shared_down_w, L0_ffn_expert_gate_up_w, L0_ffn_expert_down_w)
    return x

_drawn_inputs = setup_inputs


def setup_inputs(seed=0):
    import zlib

    import numpy as np

    out = dict(_drawn_inputs(seed))
    spreads = {'L0_attn_ln_g': (1.0, 0.6),
     'L0_attn_ln_b': (0.0, 0.8),
     'L0_attn_conv_b': (0.0, 0.8),
     'L0_attn_dt_proj_b': (-4.599999904632568, 0.6),
     'L0_attn_D': (1.0, 0.6),
     'L0_attn_glu_b': (0.0, 2.0)}
    factors = {'L0_attn_in_proj_w': 8.0,
     'L0_attn_conv_w': 8.0,
     'L0_attn_x_proj_w': 8.0,
     'L0_attn_dt_proj_w': 8.0,
     'L0_attn_A_log': 8.0,
     'L0_attn_out_proj_w': 8.0,
     'L0_attn_glu_w': 8.0,
     'L0_ffn_gate_w': 31.326,
     'L0_ffn_expert_gate_up_w': 28.235,
     'L0_ffn_expert_down_w': 28.307,
     'L0_ffn_shared_gate_w': 8.0,
     'L0_ffn_shared_gate_up_w': 8.0,
     'L0_ffn_shared_down_w': 8.0}
    for name, (base, spread) in spreads.items():
        noise = np.random.default_rng([zlib.crc32(name.encode()), seed]).standard_normal(out[name].shape)
        drawn = base * np.exp(spread * noise) if base else spread * noise
        out[name] = jnp.asarray(drawn.astype(out[name].dtype))
    for name, factor in factors.items():
        out[name] = (out[name] * factor).astype(out[name].dtype)
    return out
```

```python
from contextlib import ExitStack

import concourse.bass as bass
from concourse import mybir

F32 = mybir.dt.float32
BF16 = mybir.dt.bfloat16
I32 = mybir.dt.int32
ACT = mybir.ActivationFunctionType
ALU = mybir.AluOpType
AX = mybir.AxisListType

P = 128
B, L, DM = 32, 512, 256
T = B * L
NT = L // P
FM = DM // P
DI = 2 * DM
J = DI // P
N = 16
R = 16
TAPS = 4
PAD = TAPS - 1
E, CAP, TOPK = 64, 128, 8
IS = 512
KS = IS // P
IE = 128
ROW = DM + E
TILES = T // P
EPS = 1e-5
HR = 4
PREP_T, PREP_X, PREP_Z, PREP_S, PREP_D, PREP_USES = 0, 2, 6, 10, 11, 15
(POST_M, POST_G, POST_V, POST_MT, POST_XT, POST_R, POST_C,
 POST_SG, POST_SU, POST_DN, POST_USES) = (0, 1, 2, 3, 4, 5, 6, 7, 9, 11, 12)


def mamba_moe(nc, x, vectors, in_wT, conv_w, x_wT, dt_wT, a_log, out_wT, glu_wT, router_w, sgu_w, sdown_w, egu_w, edown_w, out, counts, table, ends):
    ctx = ExitStack()
    with ctx:
        def sb(name, shape, dt=F32):
            return ctx.enter_context(nc.sbuf_tensor(name, shape, dt))

        def sem(name):
            return ctx.enter_context(nc.semaphore(name))

        ident = sb("ident", [P, P])
        onehot = sb("onehot", [P, 2 * N], BF16)
        steps_tri = sb("steps_tri", [P, 3 * P + L], BF16)
        slot = sb("slot", [P, 1])
        slot_pad = sb("slot_pad", [P, 1])
        row_of = sb("row_of", [P, E])
        d_diag = sb("d_diag", [P, J, P])
        neg_a = sb("neg_a", [P, J, N])
        vecs = sb("vecs", [P, 20])
        g_sb, b_sb = vecs[:, 0:2], vecs[:, 2:4]
        cb_sb, db_sb, d_sb = vecs[:, 4:8], vecs[:, 8:12], vecs[:, 12:16]
        gb_sb = vecs[:, 16:20]
        cw_sb = sb("cw_sb", [P, J, TAPS])
        w_in = sb("w_in", [P, FM, 2 * DI])
        w_x = sb("w_x", [P, J, P])
        w_dt = sb("w_dt", [2 * R, DI])
        w_out = sb("w_out", [P, J, DM])
        w_glu = sb("w_glu", [P, FM, 2 * DM])
        w_r = sb("w_r", [P, FM, E + 1])
        w_sgu = sb("w_sgu", [P, FM, 2 * IS])
        w_sd = sb("w_sd", [P, KS, DM])

        decay = sb("decay", [P, 2, J, L])
        hs = sb("hs", [P, HR, J, L])
        b_all = sb("b_all", [P, 2, L])
        c_all = sb("c_all", [P, 2, L])
        xin = sb("xin", [P, NT, DM])
        xn = sb("xn", [P, NT, DM])
        xnT = sb("xnT", [P, FM, L])
        xpad = sb("xpad", [P, J, PAD + L])
        xc = sb("xc", [P, J, L])
        xd = sb("xd", [P, L])
        parts = [sb(f"parts{h}", [P, L], BF16) for h in range(2)]
        sz = [sb(f"sz{h}", [P, J, L]) for h in range(2)]
        dt = [sb(f"dt{h}", [P, J, L]) for h in range(2)]
        dtu = [sb(f"dtu{h}", [P, J, L]) for h in range(2)]
        stats = sb("stats", [P, 3, NT, 6])
        mv = sb("mv", [P, 3, NT, 2])
        rstd = sb("rstd", [P, 3, NT])
        minus_half = sb("minus_half", [P, NT])
        xs = [sb(f"xs{h}", [P, NT, DM]) for h in range(2)]
        yz = sb("yz", [P, J, L])
        mT = sb("mT", [P, FM, L])
        rows = sb("rows", [P, NT, ROW])
        lg = sb("lg", [P, NT, E + 1])
        pr = sb("pr", [P, NT, E])
        rep = sb("rep", [P, NT, E])
        top = sb("top", [P, NT, TOPK])
        maskb = sb("maskb", [P, NT, E], BF16)
        small = sb("small", [P, 6, NT])
        cnt = [sb(f"cnt{h}", [E, L]) for h in range(2)]
        tile_ends = sb("tile_ends", [E, TILES])
        ab = xpad[:, :, PAD:PAD + L]
        sg = xn[:, :, :].rearrange("p a b -> p (a b)").rearrange("p (f l) -> p f l", f=FM)
        hid, x2T, x1 = yz, mT, xn
        negmax, esum, rsum, s8, eg, gate_s = (small[:, i, :] for i in range(6))
        tau, loc = dt[0][:, 0, 0:E], dt[0][:, 0, E:2 * E]
        idx1, idx_in, idx_out = (dt[0][:, 1, i * E:(i + 1) * E].bitcast(I32) for i in range(3))
        ER = 4
        ring_in = [sb(f"ring_in{i}", [P, 1], I32) for i in range(ER)]
        ring_out = [sb(f"ring_out{i}", [P, 1], I32) for i in range(ER)]
        big = hs[:, :, :, :].rearrange("p a j l -> p (a j l)")
        slots3 = big.rearrange("p (e t) -> p e t", e=E)
        flat = decay[:, :, :, :].rearrange("p a j l -> p (a j l)")
        ewg = [flat[:, i * 768:i * 768 + 512].rearrange("p (f n) -> p f n", f=FM) for i in range(ER)]
        ewd = [flat[:, i * 768 + 512:i * 768 + 768] for i in range(ER)]
        got = [big[:, i * ROW:(i + 1) * ROW] for i in range(ER)]
        o1 = ER * ROW
        geT = [big[:, o1 + i * DM:o1 + (i + 1) * DM].rearrange("p (f n) -> p f n", f=FM) for i in range(2)]
        o2 = o1 + 2 * DM
        act_e = [big[:, o2 + i * IE:o2 + (i + 1) * IE] for i in range(2)]
        o3 = o2 + 2 * IE
        hid_e = [big[:, o3 + i * IE:o3 + (i + 1) * IE] for i in range(2)]
        o4 = o3 + 2 * IE
        res_e = [big[:, o4 + i * DM:o4 + (i + 1) * DM] for i in range(ER)]

        ps = ctx.enter_context(nc.psum_tensor("ps", [P, 8, L], F32))
        ybank = ps[:, 0:4, :]
        bcbank = ps[:, 4, :]
        prbank = ps[:, 5, :]
        pobank = ps[:, 6:8, :]
        po_tok = pobank.rearrange("p a b -> p (a b)").rearrange("p (i d) -> p i d", i=NT)

        loaded = sem("loaded")
        consts = sem("consts")
        cleared = sem("cleared")
        made = sem("made")
        passed = sem("passed")
        x_loaded = sem("x_loaded")
        ln0, ln1, ln2 = sem("ln0"), sem("ln1"), sem("ln2")
        rstd_ready = [sem(f"rstd_ready{i}") for i in range(3)]
        prep_full, prep_read = sem("prep_full"), sem("prep_read")
        post_full, post_read = sem("post_full"), sem("post_read")
        conv_step = sem("conv_step")
        xc_ready = sem("xc_ready")
        z_ready = sem("z_ready")
        split = sem("split")
        soft = sem("soft")
        dt_ready = sem("dt_ready")
        x_summed, xs_ready = sem("x_summed"), sem("xs_ready")
        bc_full, bc_copied = sem("bc_full"), sem("bc_copied")
        decay_ready = sem("decay_ready")
        input_ready = sem("input_ready")
        state_ready = sem("state_ready")
        readout_ready = sem("readout_ready")
        summed = sem("summed")
        y_read = sem("y_read")
        route = sem("route")
        exp_ready = sem("exp_ready")
        hid_ready = sem("hid_ready")
        counts_ready = sem("counts_ready")
        rows_stored, out_stored, counts_stored = sem("rows_stored"), sem("out_stored"), sem("counts_stored")
        ends_stored, ends_back = sem("ends_stored"), sem("ends_back")
        pad_stored = sem("pad_stored")
        slot_step = sem("slot_step")
        slot_rows = sem("slot_rows")
        ring_ready, e_scattered = sem("ring_ready"), sem("e_scattered")
        e_gathered = [sem(f"e_gathered{i}") for i in range(ER)]
        e_weights = [sem(f"e_weights{i}") for i in range(ER)]
        e_t, e_tc, e_gu, e_act, e_hid, e_o, e_res = (
            sem(n) for n in ("e_t", "e_tc", "e_gu", "e_act", "e_hid", "e_o", "e_res"))

        x_v = x.rearrange("b (i p) d -> b p i d", p=P)
        out_v = out[0:T, :].rearrange("(b i p) d -> b p i d", p=P, i=NT)
        table_v = table.rearrange("(b i p) d -> b p i d", p=P, i=NT)
        counts_v = counts.rearrange("e (b l) -> b e l", l=L)

        block = ctx.enter_context(nc.Block())

        def turns(eng, turn):
            turn(0, 0, True, False)
            turn(1, 1, True, True)
            with eng.Fori(1, B // 2 - 1) as it:
                turn(it * 2, 0, True, True)
                turn(it * 2 + 1, 1, True, True)
            turn(B - 2, 0, True, True)
            turn(B - 1, 1, False, True)

        def wait(eng, s, value):
            if not (isinstance(value, int) and value <= 0):
                eng.wait_ge(s, value)

        def wait_apart(eng, s, value):
            eng.wait_ge(s, value)
            if not isinstance(value, int):
                eng.sem_inc(passed, 1)

        @block.sync
        def _(sp):
            def load_x(b):
                wait(sp, xs_ready, b)
                sp.dma_start(xin[:, :, :], at(x_v, b)).then_inc(x_loaded, 16)

            sp.dma_start(xin[:, :, :], x_v[0]).then_inc(x_loaded, 16)
            sp.wait_ge(cleared, 6)
            for dst, src in (
                (vecs[:, :], vectors),
                (w_in[:, :, :], in_wT.rearrange("(f p) n -> p f n", p=P)),
                (cw_sb[:, :, :], conv_w.rearrange("(j p) o k -> p j (o k)", p=P)),
                (w_x[:, :, 0:R], x_wT[:, 0:R].rearrange("(j p) n -> p j n", p=P)),
                (w_x[:, :, 32:64], x_wT[:, R:R + 2 * N].rearrange("(j p) n -> p j n", p=P)),
                (w_x[:, :, 64:96], x_wT[:, R:R + 2 * N].rearrange("(j p) n -> p j n", p=P)),
                (w_x[:, :, 96:128], x_wT[:, R:R + 2 * N].rearrange("(j p) n -> p j n", p=P)),
                (w_dt[0:R, :], dt_wT),
                (neg_a[:, :, :], a_log.rearrange("(j p) n -> p j n", p=P)),
                (w_out[:, :, :], out_wT.rearrange("(j p) n -> p j n", p=P)),
                (w_glu[:, :, :], glu_wT.rearrange("(f p) n -> p f n", p=P)),
                (w_r[:, :, :], router_w.rearrange("(f p) n -> p f n", p=P)),
                (w_sgu[:, :, :], sgu_w.rearrange("(f p) n -> p f n", p=P)),
                (w_sd[:, :, :], sdown_w.rearrange("(k p) n -> p k n", p=P)),
            ):
                sp.dma_start(dst, src).then_inc(loaded, 16)

            def at(v, q):
                return v[q] if isinstance(q, int) else v[bass.ds(q, 1)].squeeze(0)

            def turn(b, h, prep, post):
                if not isinstance(b, int) or b + 2 < B:
                    load_x(b + 2)
                if post:
                    store(b - 1, 1 - h)

            def store(q, h):
                sp.wait_ge(post_read, q * POST_USES + POST_C + 1)
                sp.dma_start(at(counts_v, q), cnt[h][:, :]).then_inc(counts_stored, 16)
                sp.wait_ge(route, ROUTES * q + ROUTES)
                sp.dma_start(at(table_v, q), rows[:, :, :]).then_inc(rows_stored, 16)
                sp.wait_ge(post_read, q * POST_USES + POST_USES)
                sp.dma_start(at(out_v, q), x1[:, :, :]).then_inc(out_stored, 16)

            load_x(1)
            turns(sp, turn)
            store(B - 1, 1)
            sp.wait_ge(consts, CONSTS)
            sp.dma_start(out[T:T + CAP, :], xd[:, 0:DM]).then_inc(pad_stored, 16)
            sp.wait_ge(counts_ready, B)
            sp.dma_start(ends.rearrange("(e t) -> e t", t=TILES), tile_ends[:, :]).then_inc(ends_stored, 16)
            sp.wait_ge(ends_stored, 16)
            sp.wait_ge(summed, B * N)
            sp.dma_start(big, ends.rearrange("(a n) -> a n", a=1).broadcast_to([P, E * TILES]))\
                .then_inc(ends_back, 16)
            sp.wait_ge(state_ready, B * N)

            def weights(e, r):
                wait(sp, e_o, e - ER + 1)
                a, d = (egu_w[e], edown_w[e]) if isinstance(e, int) else (
                    egu_w[bass.ds(e, 1)].squeeze(0), edown_w[bass.ds(e, 1)].squeeze(0))
                sp.dma_start(ewg[r], a.rearrange("(f p) n -> p f n", p=P)).then_inc(e_weights[r], 16)
                sp.dma_start(ewd[r], d).then_inc(e_weights[r], 16)

            for e in range(ER):
                weights(e, e)
            with sp.Fori(1, E // ER) as it:
                for r in range(ER):
                    weights(it * ER + r, r)
            sp.wait_ge(rows_stored, 16 * B)
            sp.wait_ge(out_stored, 16 * B)
            sp.wait_ge(counts_stored, 16 * B)
            sp.wait_ge(pad_stored, 16)
            sp.wait_ge(e_scattered, 16 * E)

        @block.gpsimd
        def _(pool):
            pool.memset(ident[:, :], 0.0).then_inc(cleared, 1)
            pool.memset(onehot[:, :], 0.0).then_inc(cleared, 1)
            pool.memset(steps_tri[:, :], 1.0).then_inc(cleared, 1)
            pool.memset(w_x[:, :, R:32], 0.0).then_inc(cleared, 1)
            pool.memset(w_dt[:, :], 0.0).then_inc(cleared, 1)
            pool.memset(minus_half[:, :], -0.5).then_inc(cleared, 1)
            pool.wait_ge(cleared, 6)
            pool.affine_select(out=ident[:, :], in_=ident[:, :], compare_op=ALU.not_equal, fill=1.0,
                               base=0, pattern=[[-1, P]], channel_multiplier=1).then_inc(consts, 1)
            for c in range(1, 4):
                if c > 1:
                    pool.wait_ge(consts, c)
                pool.affine_select(out=onehot[:, :], in_=onehot[:, :], compare_op=ALU.not_equal, fill=1.0,
                                   base=-32 * c, pattern=[[-1, 2 * N]], channel_multiplier=1).then_inc(consts, 1)
            pool.affine_select(out=steps_tri[:, :], in_=steps_tri[:, :], compare_op=ALU.is_ge, fill=0.0,
                               base=-3 * P, pattern=[[1, 3 * P + L]], channel_multiplier=-1).then_inc(consts, 1)
            pool.iota(slot[:, :], pattern=[[0, 1]], base=0, channel_multiplier=1,
                      allow_small_or_imprecise_dtypes=True).then_inc(consts, 1)
            pool.iota(slot_pad[:, :], pattern=[[0, 1]], base=T, channel_multiplier=1,
                      allow_small_or_imprecise_dtypes=True).then_inc(consts, 1)
            pool.iota(row_of[:, :], pattern=[[TILES, E]], base=0, channel_multiplier=0,
                      allow_small_or_imprecise_dtypes=True).then_inc(consts, 1)

            def scan_input(b, h, n):
                g = b * N + n
                if n == 0:
                    pool.wait_ge(dt_ready, 2 * b + 2)
                pool.wait_ge(bc_copied, g * 2 + 1)
                wait(pool, summed, g - HR + 1)
                pool.tensor_tensor(hs[:, n % HR], dtu[h][:, :, :],
                                   b_all[:, n % 2, :].unsqueeze(1).broadcast_to([P, J, L]), ALU.mult)\
                    .then_inc(input_ready, 1)

            def scales(s, which, k):
                wait_apart(pool, s, 3 * k + 2)
                pool.tensor_scalar(rstd[:, which, :].unsqueeze(2), mv[:, which, :, 1:2], EPS, None, ALU.add)\
                    .then_inc(rstd_ready[which], 1)
                pool.wait_ge(rstd_ready[which], 2 * k + 1)
                pool.tensor_tensor(rstd[:, which, :], rstd[:, which, :], minus_half[:, :], ALU.pow)\
                    .then_inc(rstd_ready[which], 1)

            def keep_x(p, h):
                pool.wait_ge(x_summed, p + 1)
                if not (isinstance(p, int) and p < 2):
                    wait_apart(pool, post_read, (p - 2) * POST_USES + POST_MT + 1)
                pool.tensor_copy(xs[h][:, :, :], xin[:, :, :]).then_inc(xs_ready, 1)

            def split_bc(p, h):
                wait_apart(pool, prep_read, PREP_USES * p + PREP_S + 1)
                pool.tensor_copy(parts[h][:, :], xd[:, :]).then_inc(split, 1)
                pool.wait_ge(split, 4 * p + 1)
                pool.tensor_tensor(xd[64:128, :], xd[64:128, :], parts[h][64:128, :], ALU.subtract).then_inc(split, 1)
                wait_apart(pool, split, 4 * p + 2)
                pool.tensor_copy(parts[h][64:128, :], xd[64:128, :]).then_inc(split, 1)
                pool.wait_ge(split, 4 * p + 3)
                pool.tensor_tensor(parts[h][96:128, :], xd[96:128, :], parts[h][96:128, :], ALU.subtract)\
                    .then_inc(split, 1)
                pool.wait_ge(split, 4 * p + 4)

            def step_sizes(p, h):
                pool.wait_ge(soft, 2 * p + 2)
                pool.tensor_tensor(dt[h][:, :, :], dt[h][:, :, :], ab, ALU.add).then_inc(dt_ready, 1)
                pool.wait_ge(dt_ready, 2 * p + 1)
                pool.tensor_tensor(dtu[h][:, :, :], dt[h][:, :, :], xc[:, :, :], ALU.mult).then_inc(dt_ready, 1)

            def turn(b, h, prep, post):
                for n in range(N):
                    if prep and n == 1:
                        scales(ln0, 0, b + 1)
                    if prep and n == 2:
                        scales(ln1, 1, b + 1)
                    if post and n == LN2_SLOT:
                        scales(ln2, 2, b - 1)
                    if n < N - 1:
                        scan_input(b, h, n + 1)
                    elif prep:
                        scan_input(b + 1, 1 - h, 0)
                    if prep and n == XS_SLOT:
                        keep_x(b + 1, 1 - h)
                    if prep and n == SPLIT_SLOT:
                        split_bc(b + 1, 1 - h)
                    if prep and n == STEP_SLOT:
                        step_sizes(b + 1, 1 - h)

            scales(ln0, 0, 0)
            scales(ln1, 1, 0)
            keep_x(0, 0)
            split_bc(0, 0)
            step_sizes(0, 0)
            scan_input(0, 0, 0)
            turns(pool, turn)
            scales(ln2, 2, B - 1)

            pool.wait_ge(split, 4 * B)
            pool.wait_ge(prep_full, B * PREP_USES)
            pool.memset(xd[:, 0:DM], 0.0).then_inc(consts, 1)
            pool.wait_ge(slot_step, 4)
            pool.wait_ge(counts_stored, 16 * B)
            tiles = counts.rearrange("e (t k) -> (e t) k", k=P)
            for e in range(E):
                pool.indirect_dma_start(out=slots3[:, e, :], out_offset=None, in_=tiles,
                                        in_offset=bass.IndirectOffsetOnAxis(ap=idx1[:, e:e + 1], axis=0))\
                    .then_inc(slot_rows, 16)
            pool.wait_ge(rows_stored, 16 * B)
            pool.wait_ge(out_stored, 16 * B)
            pool.wait_ge(pad_stored, 16)

            def gather(e, r):
                pool.wait_ge(ring_ready, e + 1)
                if not (isinstance(e, int) and e < ER):
                    wait_apart(pool, e_res, e - ER + 1)
                pool.indirect_dma_start(out=got[r], out_offset=None, in_=table,
                                        in_offset=bass.IndirectOffsetOnAxis(ap=ring_in[r][:, :], axis=0))\
                    .then_inc(e_gathered[r], 16)

            def scatter(e, r):
                pool.wait_ge(e_res, e + 1)
                if not (isinstance(e, int) and e == 0):
                    wait_apart(pool, e_scattered, e * 16)
                pool.indirect_dma_start(out=out, out_offset=bass.IndirectOffsetOnAxis(ap=ring_out[r][:, :], axis=0),
                                        in_=res_e[r], in_offset=None, compute_op=ALU.add).then_inc(e_scattered, 16)

            AHEAD = 2
            for e in range(AHEAD):
                gather(e, e)
            for e in range(ER):
                gather(e + AHEAD, (e + AHEAD) % ER)
                scatter(e, e)
            with pool.Fori(1, E // ER - 1) as it:
                for r in range(ER):
                    gather(it * ER + r + AHEAD, (r + AHEAD) % ER)
                    scatter(it * ER + r, r)
            for e in range(E - ER, E):
                if e + AHEAD < E:
                    gather(e + AHEAD, (e + AHEAD) % ER)
                scatter(e, e % ER)
            pool.wait_ge(e_scattered, 16 * E)

        @block.scalar
        def _(act):
            act.wait_ge(loaded, 16 * LOADS)
            act.activation(neg_a[:, :, :], neg_a[:, :, :], ACT.Exp).then_inc(made, 1)

            def copy_b(g, n):
                act.wait_ge(bc_full, g * 2 + 1)
                wait(act, input_ready, g - 1)
                act.copy(b_all[:, n % 2, :], bcbank).then_inc(bc_copied, 1)

            def copy_c(g, n):
                act.wait_ge(bc_full, g * 2 + 2)
                wait(act, readout_ready, g - 1)
                act.copy(c_all[:, n % 2, :], bcbank).then_inc(bc_copied, 1)

            def decays(b, h, n):
                g = b * N + n
                if n == 0:
                    act.wait_ge(dt_ready, 2 * b + 1)
                wait(act, state_ready, g - 1)
                for j in range(J):
                    i = act.activation(decay[:, n % 2, j, 1:L], dt[h][:, j, 1:L], ACT.Exp, scale=neg_a[:, j, n:n + 1])
                i.then_inc(decay_ready, 1)

            def read_xnT(p):
                for f in range(FM):
                    act.wait_ge(prep_full, p * PREP_USES + PREP_T + f + 1)
                    act.activation(xnT[:, f, :], prbank, ACT.Identity, bias=b_sb[:, f:f + 1],
                                   scale=g_sb[:, f:f + 1]).then_inc(prep_read, 1)

            def read_xp(p, j):
                act.wait_ge(prep_full, p * PREP_USES + PREP_X + j + 1)
                wait(act, dt_ready, 2 * p)
                act.copy(xpad[:, j, PAD:PAD + L], prbank).then_inc(prep_read, 1)

            def read_z(p, h, j):
                act.wait_ge(prep_full, p * PREP_USES + PREP_Z + j + 1)
                wait(act, y_read, p - 1)
                act.copy(sz[h][:, j, :], prbank).then_inc(prep_read, 1)

            def silus(p, h):
                act.wait_ge(prep_read, p * PREP_USES + PREP_Z + J)
                act.wait_ge(conv_step, (p + 1) * J * TAPS)
                act.activation(xc[:, :, :], xc[:, :, :], ACT.Silu).then_inc(xc_ready, 1)
                act.activation(sz[h][:, :, :], sz[h][:, :, :], ACT.Silu).then_inc(z_ready, 1)

            def read_xd(p):
                act.wait_ge(prep_full, p * PREP_USES + PREP_S + 1)
                wait(act, split, 4 * p)
                act.copy(xd[:, :], prbank).then_inc(prep_read, 1)

            def read_dt(p, h, j):
                act.wait_ge(prep_full, p * PREP_USES + PREP_D + j + 1)
                wait(act, state_ready, (p - 1) * N)
                act.activation(ab[:, j, :], prbank, ACT.Abs, bias=db_sb[:, j:j + 1])
                act.activation(dt[h][:, j, :], prbank, ACT.Relu, bias=db_sb[:, j:j + 1]).then_inc(prep_read, 1)

            def softplus(p):
                act.wait_ge(prep_read, p * PREP_USES + PREP_USES)
                act.activation(ab, ab, ACT.Exp, scale=-1.0).then_inc(soft, 1)
                act.wait_ge(soft, 2 * p + 1)
                act.activation(ab, ab, ACT.Ln, bias=1.0).then_inc(soft, 1)

            def gelu(q):
                act.wait_ge(post_full, q * POST_USES + POST_M + 1)
                act.activation(mT[:, :, :], pobank, ACT.Gelu).then_inc(post_read, 1)

            def glu_gate(q):
                wait(act, out_stored, 16 * q)
                act.wait_ge(post_full, q * POST_USES + POST_G + 1)
                for f in range(FM):
                    i = act.activation(sg[:, f, :], pobank[:, f, :], ACT.Sigmoid, bias=gb_sb[:, FM + f:FM + f + 1])
                i.then_inc(post_read, 1)

            def read_x2T(q):
                act.wait_ge(post_full, q * POST_USES + POST_XT + 1)
                act.copy(x2T[:, :, :], pobank).then_inc(post_read, 1)

            def router_exp(q):
                act.wait_ge(route, q * ROUTES + 2)
                for i in range(NT):
                    act.activation(pr[:, i, :], lg[:, i, 0:E], ACT.Exp, bias=negmax[:, i:i + 1],
                                   accum_out=esum[:, i:i + 1])
                act.activation(eg.unsqueeze(2), lg[:, :, E:E + 1], ACT.Exp, scale=-1.0).then_inc(exp_ready, 1)

            def read_counts(q, h):
                act.wait_ge(post_full, q * POST_USES + POST_C + 1)
                wait(act, counts_stored, 16 * q)
                act.wait_ge(made, MADE)
                act.activation(cnt[h][:, :], pobank[0:E, 0, :], ACT.Identity, bias=cnt[1 - h][:, L - 1:L])\
                    .then_inc(post_read, 1)
                act.wait_ge(post_read, q * POST_USES + POST_C + 1)
                act.copy(tile_ends[:, bass.ds(q * NT, NT)], cnt[h][:, P - 1:L:P]).then_inc(counts_ready, 1)

            def read_gates(q, k):
                act.wait_ge(post_full, q * POST_USES + POST_SG + k + 1)
                act.copy(hid[:, 2 * k:2 * k + 2, :], pobank).then_inc(post_read, 1)

            def hid_silu(q):
                act.wait_ge(post_read, q * POST_USES + POST_SG + 2)
                act.activation(hid[:, :, :], hid[:, :, :], ACT.Silu).then_inc(hid_ready, 1)

            def turn(b, h, prep, post):
                p, q = b + 1, b - 1
                for n in range(N):
                    g = b * N + n
                    if n < N - 2:
                        copy_b(g + 2, n)
                    elif prep:
                        copy_b(g + 2, n)
                    if n < N - 1:
                        decays(b, h, n + 1)
                    elif prep:
                        decays(b + 1, 1 - h, 0)
                    if prep:
                        if n == T_SLOT:
                            read_xnT(p)
                        for j in X_SLOTS.get(n, ()):
                            read_xp(p, j)
                        for j in Z_SLOTS.get(n, ()):
                            read_z(p, 1 - h, j)
                    if n < N - 2 or prep:
                        copy_c(g + 2, n)
                    if prep:
                        if n == SILU_SLOT:
                            silus(p, 1 - h)
                        if n == XD_SLOT:
                            read_xd(p)
                        if n in D_SLOTS:
                            for j in D_SLOTS[n]:
                                read_dt(p, 1 - h, j)
                        if n == SOFT_SLOT:
                            softplus(p)
                    if post:
                        post_act(q, 1 - h, n)

            def post_act(q, h, n):
                if n == M_SLOT:
                    gelu(q)
                if n == G_SLOT:
                    glu_gate(q)
                if n == XT_SLOT:
                    read_x2T(q)
                if n == RE_SLOT:
                    router_exp(q)
                if n == C_SLOT:
                    read_counts(q, h)
                if n == SG_SLOT:
                    read_gates(q, 0)
                if n == SG_SLOT + 1:
                    read_gates(q, 1)
                if n == HID_SLOT:
                    hid_silu(q)

            act.wait_ge(made, MADE)
            read_xnT(0)
            for j in range(J):
                read_xp(0, j)
            for j in range(J):
                read_z(0, 0, j)
            silus(0, 0)
            read_xd(0)
            for j in range(J):
                read_dt(0, 0, j)
            softplus(0)
            copy_b(0, 0)
            copy_c(0, 0)
            decays(0, 0, 0)
            copy_b(1, 1)
            copy_c(1, 1)
            turns(act, turn)
            for n in range(N):
                post_act(B - 1, (B - 1) % 2, n)

            def expert(e, r, first):
                act.wait_ge(e_t, e + 1)
                if not first:
                    act.wait_ge(e_gu, e - 1)
                act.copy(geT[r % 2], ps[:, r % 2, 0:DM].rearrange("p (f n) -> p f n", f=FM)).then_inc(e_tc, 1)
                act.wait_ge(e_gu, e + 1)
                if not first:
                    act.wait_ge(e_hid, e - 1)
                act.activation(act_e[r % 2], ps[:, 2 + r % 2, 0:IE], ACT.Silu).then_inc(e_act, 1)

            for e in range(2):
                expert(e, e, True)
            for e in range(2, ER):
                expert(e, e, False)
            with act.Fori(1, E // ER) as it:
                for r in range(ER):
                    expert(it * ER + r, r, False)

        @block.tensor
        def _(pe):
            def broadcast(g, h, n, c):
                wait(pe, bc_copied, g * 2 + c)
                pe.matmul(bcbank, onehot[:, c * N + n:c * N + n + 1].broadcast_to([P, P]), parts[h][:, :],
                          start=True, stop=True).then_inc(bc_full, 1)

            def start_y(b):
                pe.wait_ge(xc_ready, b + 1)
                wait(pe, y_read, b)
                for j in range(J):
                    pe.matmul(ybank[:, j, :], d_diag[:, j, :], xc[:, j, :], start=True, stop=False)

            def sum_states(g, n):
                pe.wait_ge(readout_ready, g + 1)
                for j in range(J):
                    i = pe.matmul(ybank[:, j, :], ident[:, :], hs[:, n % HR, j, :], start=False, stop=(n == N - 1))
                i.then_inc(summed, 1)

            def use_prep(p, u):
                wait(pe, prep_read, p * PREP_USES + u)

            def turn_xn(p, f):
                pe.wait_ge(ln1, 3 * p + 3)
                use_prep(p, PREP_T + f)
                for i in range(NT):
                    m = pe.transpose(prbank[:, i * P:(i + 1) * P], xn[:, i, f * P:(f + 1) * P], ident[:, :])
                m.then_inc(prep_full, 1)

            def project_in(p, u, col):
                pe.wait_ge(prep_read, p * PREP_USES + PREP_T + FM)
                use_prep(p, u)
                for f in range(FM):
                    m = pe.matmul(prbank, w_in[:, f, col * P:(col + 1) * P], xnT[:, f, :],
                                  start=(f == 0), stop=(f == FM - 1))
                m.then_inc(prep_full, 1)

            def project_x(p):
                pe.wait_ge(xc_ready, p + 1)
                use_prep(p, PREP_S)
                for j in range(J):
                    m = pe.matmul(prbank, w_x[:, j, :], xc[:, j, :], start=(j == 0), stop=(j == J - 1))
                m.then_inc(prep_full, 1)

            def project_dt(p, j):
                use_prep(p, PREP_D + j)
                pe.matmul(prbank, w_dt[:, j * P:(j + 1) * P], xd[0:2 * R, :], start=True, stop=True)\
                    .then_inc(prep_full, 1)

            def use_post(q, u):
                wait(pe, post_read, q * POST_USES + u)

            def project_out(q):
                pe.wait_ge(y_read, q + 1)
                use_post(q, POST_M)
                for f in range(FM):
                    for j in range(J):
                        m = pe.matmul(pobank[:, f, :], w_out[:, j, f * P:(f + 1) * P], yz[:, j, :],
                                      start=(j == 0), stop=(j == J - 1))
                m.then_inc(post_full, 1)

            def project_glu(q, u, half):
                use_post(q, u)
                for f in range(FM):
                    for k in range(FM):
                        col = (half * FM + f) * P
                        m = pe.matmul(pobank[:, f, :], w_glu[:, k, col:col + P], mT[:, k, :],
                                      start=(k == 0), stop=(k == FM - 1))
                m.then_inc(post_full, 1)

            def turn_m(q):
                use_post(q, POST_MT)
                for i in range(NT):
                    for f in range(FM):
                        m = pe.transpose(po_tok[:, i, f * P:(f + 1) * P], sg[:, f, i * P:(i + 1) * P], ident[:, :])
                m.then_inc(post_full, 1)

            def turn_x2(q):
                pe.wait_ge(ln2, 3 * q + 3)
                use_post(q, POST_XT)
                for f in range(FM):
                    for i in range(NT):
                        m = pe.transpose(pobank[:, f, i * P:(i + 1) * P], rows[:, i, f * P:(f + 1) * P], ident[:, :])
                m.then_inc(post_full, 1)

            def logits(q):
                use_post(q, POST_R)
                for i in range(NT):
                    for f in range(FM):
                        m = pe.matmul(pobank[:, 0, i * P:i * P + E + 1], x2T[:, f, i * P:(i + 1) * P], w_r[:, f, :],
                                      start=(f == 0), stop=(f == FM - 1))
                m.then_inc(post_full, 1)

            def count(q):
                pe.wait_ge(route, q * ROUTES + MASK_STEP)
                use_post(q, POST_C)
                for i in range(NT):
                    at = (NT - 1 - i) * P
                    m = pe.matmul(pobank[0:E, 0, :], maskb[:, i, :], steps_tri[:, at:at + L],
                                  start=(i == 0), stop=(i == NT - 1))
                m.then_inc(post_full, 1)

            def shared_up(q, u, first):
                use_post(q, u)
                for k in range(2):
                    for f in range(FM):
                        col = (first + k) * P
                        m = pe.matmul(pobank[:, k, :], w_sgu[:, f, col:col + P], x2T[:, f, :],
                                      start=(f == 0), stop=(f == FM - 1))
                m.then_inc(post_full, 1)

            def shared_down(q):
                use_post(q, POST_DN)
                for i in range(NT):
                    for k in range(KS):
                        m = pe.matmul(po_tok[:, i, :], hid[:, k, i * P:(i + 1) * P], w_sd[:, k, :],
                                      start=(k == 0), stop=(k == KS - 1))
                m.then_inc(post_full, 1)

            def post_pe(q, n):
                if n == M_SLOT:
                    project_out(q)
                if n == G_SLOT:
                    project_glu(q, POST_G, 1)
                if n == V_SLOT:
                    project_glu(q, POST_V, 0)
                if n == MT_SLOT:
                    turn_m(q)
                if n == XT_SLOT:
                    turn_x2(q)
                if n == R_SLOT:
                    logits(q)
                if n == C_SLOT:
                    count(q)
                if n == SG_SLOT:
                    shared_up(q, POST_SG, 0)
                if n == SG_SLOT + 1:
                    shared_up(q, POST_SG + 1, 2)
                if n == SU_SLOT:
                    shared_up(q, POST_SU, KS)
                if n == SU_SLOT + 1:
                    shared_up(q, POST_SU + 1, KS + 2)
                if n == DN_SLOT:
                    shared_down(q)

            def turn(b, h, prep, post):
                p, q = b + 1, b - 1
                for n in range(N):
                    g = b * N + n
                    inside = n < N - 2
                    hn, nn = (h, n + 2) if inside else (1 - h, n + 2 - N)
                    if inside or prep:
                        broadcast(g + 2, hn, nn, 0)
                    if prep:
                        if n == T_SLOT:
                            turn_xn(p, 0)
                            turn_xn(p, 1)
                        for j in X_SLOTS.get(n, ()):
                            project_in(p, PREP_X + j, j)
                        for j in Z_SLOTS.get(n, ()):
                            project_in(p, PREP_Z + j, J + j)
                    if inside or prep:
                        broadcast(g + 2, hn, nn, 1)
                    if prep:
                        if n == XD_SLOT:
                            project_x(p)
                        if n in D_SLOTS:
                            if n == min(D_SLOTS):
                                pe.wait_ge(prep_read, p * PREP_USES + PREP_S + 1)
                            for j in D_SLOTS[n]:
                                project_dt(p, j)
                    if post:
                        post_pe(q, n)
                    if n == 0:
                        start_y(b)
                    sum_states(g, n)

            pe.wait_ge(loaded, 16 * LOADS)
            pe.wait_ge(consts, 8)
            pe.wait_ge(made, MADE)
            turn_xn(0, 0)
            turn_xn(0, 1)
            for j in range(J):
                project_in(0, PREP_X + j, j)
            for j in range(J):
                project_in(0, PREP_Z + j, J + j)
            project_x(0)
            for j in range(J):
                project_dt(0, j)
            pe.wait_ge(split, 4)
            for n in range(2):
                for c in range(2):
                    broadcast(n, 0, n, c)
            turns_pe = turn
            turns(pe, turns_pe)
            for n in range(N):
                post_pe(B - 1, n)

            def expert(e, r, first):
                pe.wait_ge(e_gathered[r], (e // ER + 1) * 16 if isinstance(e, int) else e_turn(e, r))
                if not first:
                    pe.wait_ge(e_tc, e - 1)
                for f in range(FM):
                    m = pe.transpose(ps[:, r % 2, f * P:(f + 1) * P], got[r][:, f * P:(f + 1) * P], ident[:, :])
                m.then_inc(e_t, 1)
                pe.wait_ge(e_weights[r], (e // ER + 1) * 32 if isinstance(e, int) else e_turn(e, r) * 2)
                pe.wait_ge(e_tc, e + 1)
                if not first:
                    pe.wait_ge(e_hid, e - 1)
                for half in range(2):
                    for f in range(FM):
                        m = pe.matmul(ps[:, 2 + r % 2, half * IE:(half + 1) * IE],
                                      ewg[r][:, f, half * IE:(half + 1) * IE], geT[r % 2][:, f, :],
                                      start=(f == 0), stop=(f == FM - 1))
                m.then_inc(e_gu, 1)
                pe.wait_ge(e_hid, e + 1)
                if not first:
                    pe.wait_ge(e_res, e - 1)
                pe.matmul(ps[:, 4 + r % 2, 0:DM], hid_e[r % 2], ewd[r], start=True, stop=True).then_inc(e_o, 1)

            for e in range(ER):
                expert(e, e, e < 2)
            with pe.Fori(1, E // ER) as it:
                def e_turn(e, r):
                    return it * 16 + 16
                for r in range(ER):
                    expert(it * ER + r, r, False)

        @block.vector
        def _(dve):
            for k, t in enumerate((decay[:, :, :, 0:1], xpad[:, :, 0:PAD], cnt[1][:, L - 1:L])):
                dve.memset(t, 0.0).then_inc(made, 1)
            dve.wait_ge(loaded, 16 * LOADS)
            dve.wait_ge(made, 4)
            dve.tensor_scalar(neg_a[:, :, :], neg_a[:, :, :], -1.0, None, ALU.mult).then_inc(made, 1)
            dve.wait_ge(consts, 8)
            for j in range(J):
                dve.tensor_scalar(d_diag[:, j, :], ident[:, :], d_sb[:, j:j + 1], None, ALU.mult).then_inc(made, 1)

            def moments(s, which, k, src):
                for i in range(NT):
                    m = dve.bn_stats(stats[:, which, i, :], src[:, i, :])
                m.then_inc(s, 1)
                wait_apart(dve, s, 3 * k + 1)
                for i in range(NT):
                    m = dve.bn_aggr(mv[:, which, i, :], stats[:, which, i, :])
                m.then_inc(s, 1)

            def normalise(s, which, k, src, dst):
                dve.wait_ge(rstd_ready[which], 2 * k + 2)
                for i in range(NT):
                    m = dve.tensor_scalar(dst[:, i, 0:DM], src[:, i, :], mv[:, which, i, 0:1],
                                          rstd[:, which, i:i + 1], ALU.subtract, ALU.mult)
                m.then_inc(s, 1)

            def moments_x(p):
                dve.wait_ge(x_loaded, 16 * p + 16)
                moments(ln0, 0, p, xin)

            def norm_x(p):
                wait(dve, prep_full, (p - 1) * PREP_USES + PREP_T + FM)
                wait(dve, out_stored, 16 * (p - 2))
                normalise(ln0, 0, p, xin, xn)
                dve.wait_ge(ln0, 3 * p + 3)
                dve.tensor_tensor(xin[:, :, :], xin[:, :, :], xn[:, :, :], ALU.add).then_inc(x_summed, 1)
                moments(ln1, 1, p, xn)

            def norm_again(p):
                dve.wait_ge(x_summed, p + 1)
                normalise(ln1, 1, p, xn, xn)

            def conv(p, j):
                dve.wait_ge(prep_read, p * PREP_USES + PREP_X + j + 1)
                if j == 0:
                    wait(dve, summed, (p - 1) * N + 1)
                dve.tensor_scalar(xc[:, j, :], xpad[:, j, 0:L], cw_sb[:, j, 0:1], cb_sb[:, j:j + 1],
                                  ALU.mult, ALU.add).then_inc(conv_step, 1)
                for k in range(1, TAPS):
                    dve.wait_ge(conv_step, (p * J + j) * TAPS + k)
                    dve.scalar_tensor_tensor(xc[:, j, :], xpad[:, j, k:k + L], cw_sb[:, j, k:k + 1], xc[:, j, :],
                                             ALU.mult, ALU.add).then_inc(conv_step, 1)

            def gate_y(q, h):
                dve.wait_ge(summed, (q + 1) * N)
                dve.wait_ge(z_ready, q + 1)
                wait(dve, post_full, q * POST_USES)
                dve.tensor_tensor(yz[:, :, :], ybank, sz[h][:, :, :], ALU.mult).then_inc(y_read, 1)

            def glu(q):
                dve.wait_ge(post_full, q * POST_USES + POST_V + 1)
                dve.wait_ge(post_read, q * POST_USES + POST_G + 1)
                for f in range(FM):
                    i = dve.scalar_tensor_tensor(sg[:, f, :], pobank[:, f, :], gb_sb[:, f:f + 1], sg[:, f, :],
                                                 ALU.add, ALU.mult)
                i.then_inc(post_read, 1)

            def add_m(q, h):
                dve.wait_ge(post_full, q * POST_USES + POST_MT + 1)
                dve.wait_ge(xs_ready, q + 1)
                dve.tensor_tensor(x1[:, :, :], po_tok, xs[h][:, :, :], ALU.add).then_inc(post_read, 1)

            def moments_x1(q):
                dve.wait_ge(post_read, q * POST_USES + POST_MT + 1)
                moments(ln2, 2, q, x1)

            def norm_x1(q):
                wait(dve, rows_stored, 16 * q)
                normalise(ln2, 2, q, x1, rows)

            def read_logits(q):
                dve.wait_ge(post_full, q * POST_USES + POST_R + 1)
                dve.tensor_copy(lg[:, :, :], pobank[:, 0, :].rearrange("p (i c) -> p i c", i=NT)[:, :, 0:E + 1])\
                    .then_inc(post_read, 1)
                dve.wait_ge(post_read, q * POST_USES + POST_R + 1)
                dve.tensor_reduce(negmax, lg[:, :, 0:E], AX.X, ALU.max, negate=True).then_inc(route, 2)

            def choose(q):
                at = [q * ROUTES + 2]

                def link(i):
                    i.then_inc(route, 1)
                    at[0] = at[0] + 1
                    wait_apart(dve, route, at[0])

                def wide(t, w):
                    return t.unsqueeze(2).broadcast_to([P, NT, w])

                dve.wait_ge(exp_ready, q + 1)
                dve.reciprocal(rsum, esum)
                link(dve.tensor_scalar(gate_s, eg, 1.0, None, ALU.add))
                dve.reciprocal(gate_s, gate_s)
                link(dve.tensor_tensor(pr[:, :, :], pr[:, :, :], wide(rsum, E), ALU.mult))
                for i in range(NT):
                    k = dve.max(top[:, i, :], pr[:, i, :])
                link(k)
                for i in range(NT):
                    dve.match_replace(rep[:, i, :], top[:, i, :], pr[:, i, :], -1.0)
                link(dve.tensor_reduce(s8, top[:, :, :], AX.X, ALU.add))
                dve.reciprocal(s8, s8)
                link(dve.tensor_tensor(rep[:, :, :], rep[:, :, :], pr[:, :, :], ALU.not_equal))
                link(dve.tensor_copy(maskb[:, :, :], rep[:, :, :]))
                link(dve.tensor_tensor(pr[:, :, :], pr[:, :, :], rep[:, :, :], ALU.mult))
                dve.tensor_tensor(rows[:, :, DM:ROW], pr[:, :, :], wide(s8, E), ALU.mult).then_inc(route, 1)

            def mul_up(q, k):
                dve.wait_ge(post_full, q * POST_USES + POST_SU + k + 1)
                if k == 0:
                    dve.wait_ge(hid_ready, q + 1)
                dve.tensor_tensor(hid[:, 2 * k:2 * k + 2, :], pobank, hid[:, 2 * k:2 * k + 2, :], ALU.mult)\
                    .then_inc(post_read, 1)

            def add_shared(q, h):
                dve.wait_ge(post_full, q * POST_USES + POST_DN + 1)
                for i in range(NT):
                    k = dve.scalar_tensor_tensor(x1[:, i, :], po_tok[:, i, :], gate_s[:, i:i + 1], x1[:, i, :],
                                                 ALU.mult, ALU.add)
                k.then_inc(post_read, 1)

            def post_dve(q, h, n):
                if n == V_SLOT:
                    glu(q)
                if n == MT_SLOT:
                    add_m(q, h)
                    moments_x1(q)
                if n == LN2_SLOT:
                    norm_x1(q)
                if n == R_SLOT:
                    read_logits(q)
                if n == CH_SLOT:
                    choose(q)
                if n == SU_SLOT:
                    mul_up(q, 0)
                if n == SU_SLOT + 1:
                    mul_up(q, 1)
                if n == DN_SLOT:
                    add_shared(q, h)

            def turn(b, h, prep, post):
                p, q = b + 1, b - 1
                for n in range(N):
                    g = b * N + n
                    dve.wait_ge(decay_ready, g + 1)
                    dve.wait_ge(input_ready, g + 1)
                    dve.tensor_tensor_scan(hs[:, n % HR].rearrange("p j l -> p (j l)"),
                                           decay[:, n % 2].rearrange("p j l -> p (j l)"),
                                           hs[:, n % HR].rearrange("p j l -> p (j l)"), 0.0, ALU.mult, ALU.add)\
                        .then_inc(state_ready, 1)
                    if n == 0 and post:
                        gate_y(q, 1 - h)
                    dve.wait_ge(state_ready, g + 1)
                    dve.wait_ge(bc_copied, g * 2 + 2)
                    dve.tensor_tensor(hs[:, n % HR], hs[:, n % HR],
                                      c_all[:, n % 2, :].unsqueeze(1).broadcast_to([P, J, L]), ALU.mult)\
                        .then_inc(readout_ready, 1)
                    if prep:
                        if n == 0:
                            moments_x(p)
                        if n == 1:
                            norm_x(p)
                        if n == 2:
                            norm_again(p)
                        for j in CONV_SLOTS.get(n, ()):
                            conv(p, j)
                    if post:
                        post_dve(q, 1 - h, n)

            moments_x(0)
            norm_x(0)
            norm_again(0)
            for j in range(J):
                conv(0, j)
            turns(dve, turn)
            gate_y(B - 1, (B - 1) % 2)
            for n in range(N):
                post_dve(B - 1, (B - 1) % 2, n)

            dve.wait_ge(ends_back, 16)
            dve.wait_ge(consts, 8)
            dve.tensor_scalar(big, big, slot[:, 0:1], None, ALU.is_le).then_inc(slot_step, 1)
            dve.wait_ge(slot_step, 1)
            dve.tensor_reduce(tau, slots3, AX.X, ALU.add).then_inc(slot_step, 1)
            dve.wait_ge(slot_step, 2)
            dve.scalar_tensor_tensor(loc, tau, float(TILES - 1), row_of[:, :], ALU.min, ALU.add)\
                .then_inc(slot_step, 1)
            dve.wait_ge(slot_step, 3)
            dve.tensor_copy(idx1, loc).then_inc(slot_step, 1)
            dve.wait_ge(slot_rows, 16 * E)
            dve.tensor_scalar(big, big, slot[:, 0:1], None, ALU.is_le).then_inc(slot_step, 1)
            dve.wait_ge(slot_step, 5)
            dve.tensor_reduce(loc, slots3, AX.X, ALU.add).then_inc(slot_step, 1)
            dve.wait_ge(slot_step, 6)
            dve.scalar_tensor_tensor(loc, tau, float(P), loc, ALU.mult, ALU.add).then_inc(slot_step, 1)
            dve.wait_ge(slot_step, 7)
            dve.tensor_scalar(idx_in, loc, float(T - 1), None, ALU.min).then_inc(slot_step, 1)
            dve.tensor_scalar(idx_out, loc, slot_pad[:, 0:1], None, ALU.min).then_inc(slot_step, 1)
            dve.wait_ge(slot_step, 9)

            def indices(e, r):
                wait(dve, e_scattered, (e - ER + 1) * 16)
                dve.tensor_copy(ring_out[r][:, :], idx_out[:, bass.ds(e, 1)])
                dve.tensor_copy(ring_in[r][:, :], idx_in[:, bass.ds(e, 1)]).then_inc(ring_ready, 1)

            def expert(e, r, first):
                dve.wait_ge(e_act, e + 1)
                if not first:
                    dve.wait_ge(e_o, e - 1)
                dve.tensor_tensor(hid_e[r % 2], ps[:, 2 + r % 2, IE:2 * IE], act_e[r % 2], ALU.mult).then_inc(e_hid, 1)
                dve.wait_ge(e_o, e + 1)
                dve.wait_ge(ring_ready, e + 1)
                dve.tensor_scalar(res_e[r], ps[:, 4 + r % 2, 0:DM], got[r][:, bass.ds(e + DM, 1)], None, ALU.mult)\
                    .then_inc(e_res, 1)

            AHEAD = 2
            for e in range(AHEAD):
                indices(e, e)
            for e in range(ER):
                indices(e + AHEAD, (e + AHEAD) % ER)
                expert(e, e, e < 2)
            with dve.Fori(1, E // ER - 1) as it:
                for r in range(ER):
                    indices(it * ER + r + AHEAD, (r + AHEAD) % ER)
                    expert(it * ER + r, r, False)
            for e in range(E - ER, E):
                if e + AHEAD < E:
                    indices(e + AHEAD, (e + AHEAD) % ER)
                expert(e, e % ER, False)


ROUTES, MASK_STEP = 10, 8
CONSTS, MADE = 9, 9
LOADS = 14
T_SLOT = 3
X_SLOTS = {4: (0, 1), 5: (2, 3)}
CONV_SLOTS = {5: (0, 1), 6: (2, 3)}
Z_SLOTS = {6: (0, 1), 7: (2, 3)}
SILU_SLOT = 8
XS_SLOT = 8
XD_SLOT = 9
SPLIT_SLOT = 11
D_SLOTS = {10: (0, 1), 11: (2, 3)}
SOFT_SLOT = 12
STEP_SLOT = 13
M_SLOT, G_SLOT, V_SLOT, MT_SLOT, LN2_SLOT, XT_SLOT, R_SLOT, RE_SLOT, CH_SLOT, C_SLOT = 1, 3, 4, 5, 6, 7, 8, 9, 9, 10
SG_SLOT, HID_SLOT, SU_SLOT, DN_SLOT = 10, 11, 12, 14


def kernel(**inputs):
    import concourse.bacc as bacc
    import numpy as np
    from concourse.bass_utils import run_bass_kernel_spmd as run

    nc = bacc.Bacc("TRN2", target_bir_lowering=False, num_devices=1)
    a, f = "L0_attn_", "L0_ffn_"
    vectors = np.concatenate([np.asarray(inputs[a + v]).reshape(-1, P).T for v in (
        "ln_g", "ln_b", "conv_b", "dt_proj_b", "D", "glu_b")], axis=1)
    laid = {
        "x": inputs[a + "x"], "vectors": vectors,
        "in_wT": np.asarray(inputs[a + "in_proj_w"]).T, "conv_w": inputs[a + "conv_w"],
        "x_wT": np.asarray(inputs[a + "x_proj_w"]).T, "dt_wT": np.asarray(inputs[a + "dt_proj_w"]).T,
        "a_log": inputs[a + "A_log"], "out_wT": np.asarray(inputs[a + "out_proj_w"]).T,
        "glu_wT": np.asarray(inputs[a + "glu_w"]).T,
        "router_w": np.concatenate([inputs[f + "gate_w"], inputs[f + "shared_gate_w"]], axis=1),
        "sgu_w": inputs[f + "shared_gate_up_w"], "sdown_w": inputs[f + "shared_down_w"],
        "egu_w": inputs[f + "expert_gate_up_w"], "edown_w": inputs[f + "expert_down_w"],
    }
    arrays, args = {}, []
    for name, v in laid.items():
        v = np.ascontiguousarray(v)
        arrays[name] = v
        args.append(nc.dram_tensor(name, v.shape, mybir.dt.from_np(v.dtype), kind="ExternalInput").ap())
    args.append(nc.dram_tensor("out", [T + CAP, DM], F32, kind="ExternalOutput").ap())
    args.append(nc.dram_tensor("counts", [E, T], F32, kind="Internal").ap())
    args.append(nc.dram_tensor("table", [T, ROW], F32, kind="Internal").ap())
    args.append(nc.dram_tensor("ends", [E * TILES], F32, kind="Internal").ap())
    mamba_moe(nc, *args)
    r = run(nc, [arrays], core_ids=[0])
    return r.results[0]["out"][0:T].reshape(B, L, DM)
```

```python
from contextlib import ExitStack

import concourse.bass as bass
from concourse import mybir

F32 = mybir.dt.float32
BF16 = mybir.dt.bfloat16
I32 = mybir.dt.int32
ACT = mybir.ActivationFunctionType
ALU = mybir.AluOpType
AX = mybir.AxisListType

P = 128
B, L, DM = 32, 512, 256
T = B * L
NT = L // P
FM = DM // P
DI = 2 * DM
J = DI // P
N = 16
R = 16
TAPS = 4
PAD = TAPS - 1
E, CAP, TOPK = 64, 128, 8
IS = 512
KS = IS // P
IE = 128
ROW = DM + E
TILES = T // P
EPS = 1e-5
HR = 4
PREP_T, PREP_X, PREP_Z, PREP_S, PREP_D, PREP_USES = 0, 2, 6, 10, 11, 15
(POST_M, POST_G, POST_V, POST_MT, POST_XT, POST_R, POST_SG,
 POST_SG2, POST_C, POST_SU, POST_SU2, POST_DN, POST_USES) = range(13)


def mamba_moe(nc, x, vectors, in_wT, conv_w, x_wT, dt_wT, a_log, out_wT, glu_wT, router_w, sgu_w, sdown_w, egu_w, edown_w, out, counts, table, ends):
    ctx = ExitStack()
    with ctx:
        def sb(name, shape, dt=F32):
            return ctx.enter_context(nc.sbuf_tensor(name, shape, dt))

        def sem(name):
            return ctx.enter_context(nc.semaphore(name))

        ident = sb("ident", [P, P])
        onehot = sb("onehot", [P, 2 * N], BF16)
        steps_tri = sb("steps_tri", [P, 3 * P + L], BF16)
        slot = sb("slot", [P, 1])
        slot_pad = sb("slot_pad", [P, 1])
        row_of = sb("row_of", [P, E])
        d_diag = sb("d_diag", [P, J, P])
        neg_a = sb("neg_a", [P, J, N])
        vecs = sb("vecs", [P, 20])
        g_sb, b_sb = vecs[:, 0:2], vecs[:, 2:4]
        cb_sb, db_sb, d_sb = vecs[:, 4:8], vecs[:, 8:12], vecs[:, 12:16]
        gb_sb = vecs[:, 16:20]
        cw_sb = sb("cw_sb", [P, J, TAPS])
        w_in = sb("w_in", [P, FM, 2 * DI])
        w_x = sb("w_x", [P, J, P])
        w_dt = sb("w_dt", [2 * R, DI])
        w_out = sb("w_out", [P, J, DM])
        w_glu = sb("w_glu", [P, FM, 2 * DM])
        w_r = sb("w_r", [P, FM, E + 1])
        w_sgu = sb("w_sgu", [P, FM, 2 * IS])
        w_sd = sb("w_sd", [P, KS, DM])

        decay = sb("decay", [P, 2, J, L])
        hs = sb("hs", [P, HR, J, L])
        b_all = sb("b_all", [P, 2, L])
        c_all = sb("c_all", [P, 2, L])
        xin = sb("xin", [P, NT, DM])
        xn = sb("xn", [P, NT, DM])
        xnT = sb("xnT", [P, FM, L])
        xpad = sb("xpad", [P, J, PAD + L])
        xc = sb("xc", [P, J, L])
        xd = sb("xd", [P, L])
        parts = [sb(f"parts{h}", [P, L], BF16) for h in range(2)]
        sz = [sb(f"sz{h}", [P, J, L]) for h in range(2)]
        dt = [sb(f"dt{h}", [P, J, L]) for h in range(2)]
        dtu = [sb(f"dtu{h}", [P, J, L]) for h in range(2)]
        stats = sb("stats", [P, 3, NT, 6])
        mv = sb("mv", [P, 3, NT, 2])
        rstd = sb("rstd", [P, 3, NT])
        minus_half = sb("minus_half", [P, NT])
        xs = [sb(f"xs{h}", [P, NT, DM]) for h in range(2)]
        hid = sb("hid", [P, J, L])
        mT = sb("mT", [P, FM, L])
        rows = sb("rows", [P, NT, ROW])
        lg = sb("lg", [P, NT, E + 1])
        pr = sb("pr", [P, NT, E])
        rep = sb("rep", [P, NT, E])
        top = sb("top", [P, NT, TOPK])
        maskb = sb("maskb", [P, NT, E], BF16)
        small = sb("small", [P, 6, NT])
        cnt = [sb(f"cnt{h}", [E, L]) for h in range(2)]
        tile_ends = sb("tile_ends", [E, TILES])
        ab = xpad[:, :, PAD:PAD + L]
        sg = xn[:, :, :].rearrange("p a b -> p (a b)").rearrange("p (f l) -> p f l", f=FM)
        x2T, x1 = mT, xn
        outb = mT[:, :, :].rearrange("p f l -> p (f l)")
        negmax, esum, rsum, s8, eg, gate_s = (small[:, i, :] for i in range(6))
        tau, loc = dt[0][:, 0, 0:E], dt[0][:, 0, E:2 * E]
        idx1, idx_in, idx_out = (dt[0][:, 1, i * E:(i + 1) * E].bitcast(I32) for i in range(3))
        ER = 4
        ring_in = [sb(f"ring_in{i}", [P, 1], I32) for i in range(ER)]
        ring_out = [sb(f"ring_out{i}", [P, 1], I32) for i in range(ER)]
        big = hs[:, :, :, :].rearrange("p a j l -> p (a j l)")
        slots3 = big.rearrange("p (e t) -> p e t", e=E)
        flat = decay[:, :, :, :].rearrange("p a j l -> p (a j l)")
        ewg = [flat[:, i * 768:i * 768 + 512].rearrange("p (f n) -> p f n", f=FM) for i in range(ER)]
        ewd = [flat[:, i * 768 + 512:i * 768 + 768] for i in range(ER)]
        got = [big[:, i * ROW:(i + 1) * ROW] for i in range(ER)]
        o1 = ER * ROW
        geT = [big[:, o1 + i * DM:o1 + (i + 1) * DM].rearrange("p (f n) -> p f n", f=FM) for i in range(2)]
        o2 = o1 + 2 * DM
        act_e = [big[:, o2 + i * IE:o2 + (i + 1) * IE] for i in range(2)]
        o3 = o2 + 2 * IE
        hid_e = [big[:, o3 + i * IE:o3 + (i + 1) * IE] for i in range(2)]
        o4 = o3 + 2 * IE
        res_e = [big[:, o4 + i * DM:o4 + (i + 1) * DM] for i in range(ER)]

        ps = ctx.enter_context(nc.psum_tensor("ps", [P, 8, L], F32))
        ybank = ps[:, 0:4, :]
        bcbank = ps[:, 4, :]
        prbank = ps[:, 5, :]
        pobank = ps[:, 6:8, :]
        po_tok = pobank.rearrange("p a b -> p (a b)").rearrange("p (i d) -> p i d", i=NT)

        loaded = sem("loaded")
        consts = sem("consts")
        cleared = sem("cleared")
        made = sem("made")
        passed = sem("passed")
        x_loaded = sem("x_loaded")
        ln0, ln1, ln2 = sem("ln0"), sem("ln1"), sem("ln2")
        rstd_ready = [sem(f"rstd_ready{i}") for i in range(3)]
        prep_full, prep_read = sem("prep_full"), sem("prep_read")
        post_full, post_read = sem("post_full"), sem("post_read")
        conv_step = sem("conv_step")
        xc_ready = sem("xc_ready")
        z_ready = sem("z_ready")
        split = sem("split")
        soft = sem("soft")
        dt_ready = sem("dt_ready")
        x_summed, xs_ready = sem("x_summed"), sem("xs_ready")
        b_full, b_copied = sem("b_full"), sem("b_copied")
        c_full, c_copied = sem("c_full"), sem("c_copied")
        decay_ready = sem("decay_ready")
        input_ready = sem("input_ready")
        state_ready = sem("state_ready")
        readout_ready = sem("readout_ready")
        summed = sem("summed")
        y_read = sem("y_read")
        route = sem("route")
        exp_ready = sem("exp_ready")
        hid_ready = sem("hid_ready")
        counts_ready = sem("counts_ready")
        rows_stored, out_stored, counts_stored = sem("rows_stored"), sem("out_stored"), sem("counts_stored")
        ends_stored, ends_back = sem("ends_stored"), sem("ends_back")
        pad_stored = sem("pad_stored")
        slot_step = sem("slot_step")
        slot_rows = sem("slot_rows")
        ring_ready, e_scattered = sem("ring_ready"), sem("e_scattered")
        e_gathered = [sem(f"e_gathered{i}") for i in range(ER)]
        e_weights = [sem(f"e_weights{i}") for i in range(ER)]
        e_t, e_tc, e_gu, e_act, e_hid, e_o, e_res = (
            sem(n) for n in ("e_t", "e_tc", "e_gu", "e_act", "e_hid", "e_o", "e_res"))

        x_v = x.rearrange("b (i p) d -> b p i d", p=P)
        out_v = out[0:T, :].rearrange("(b i p) d -> b p i d", p=P, i=NT)
        table_v = table.rearrange("(b i p) d -> b p i d", p=P, i=NT)
        counts_v = counts.rearrange("e (b l) -> b e l", l=L)

        block = ctx.enter_context(nc.Block())

        def turns(eng, turn):
            turn(0, 0, True, False, False)
            turn(1, 1, True, True, False)
            with eng.Fori(1, B // 2 - 1) as it:
                turn(it * 2, 0, True, True, True)
                turn(it * 2 + 1, 1, True, True, True)
            turn(B - 2, 0, True, True, True)
            turn(B - 1, 1, False, True, True)

        def wait(eng, s, value):
            if not (isinstance(value, int) and value <= 0):
                eng.wait_ge(s, value)

        def wait_apart(eng, s, value):
            eng.wait_ge(s, value)
            if not isinstance(value, int):
                eng.sem_inc(passed, 1)

        @block.sync
        def _(sp):
            def load_x(b):
                sp.wait_ge(xs_ready, 16 * b)
                sp.dma_start(xin[:, :, :], at(x_v, b)).then_inc(x_loaded, 16)

            sp.dma_start(xin[:, :, :], x_v[0]).then_inc(x_loaded, 16)
            sp.wait_ge(cleared, 6)
            for dst, src in (
                (vecs[:, :], vectors),
                (w_in[:, :, :], in_wT.rearrange("(f p) n -> p f n", p=P)),
                (cw_sb[:, :, :], conv_w.rearrange("(j p) o k -> p j (o k)", p=P)),
                (w_x[:, :, 0:R], x_wT[:, 0:R].rearrange("(j p) n -> p j n", p=P)),
                (w_x[:, :, 32:64], x_wT[:, R:R + 2 * N].rearrange("(j p) n -> p j n", p=P)),
                (w_x[:, :, 64:96], x_wT[:, R:R + 2 * N].rearrange("(j p) n -> p j n", p=P)),
                (w_x[:, :, 96:128], x_wT[:, R:R + 2 * N].rearrange("(j p) n -> p j n", p=P)),
                (w_dt[0:R, :], dt_wT),
                (neg_a[:, :, :], a_log.rearrange("(j p) n -> p j n", p=P)),
                (w_out[:, :, :], out_wT.rearrange("(j p) n -> p j n", p=P)),
                (w_glu[:, :, :], glu_wT.rearrange("(f p) n -> p f n", p=P)),
                (w_r[:, :, :], router_w.rearrange("(f p) n -> p f n", p=P)),
                (w_sgu[:, :, :], sgu_w.rearrange("(f p) n -> p f n", p=P)),
                (w_sd[:, :, :], sdown_w.rearrange("(k p) n -> p k n", p=P)),
            ):
                sp.dma_start(dst, src).then_inc(loaded, 16)

            def at(v, q):
                return v[q] if isinstance(q, int) else v[bass.ds(q, 1)].squeeze(0)

            def turn(b, h, prep, post, finish):
                if finish:
                    store_out(b - 2)
                if prep:
                    keep_x(b + 1, 1 - h)
                if not isinstance(b, int) or b + 2 < B:
                    load_x(b + 2)
                if post:
                    store(b - 1, 1 - h)

            def store(q, h):
                sp.wait_ge(post_read, q * POST_USES + POST_C + 1)
                sp.dma_start(at(counts_v, q), cnt[h][:, :]).then_inc(counts_stored, 16)
                sp.wait_ge(route, ROUTES * q + ROUTES)
                sp.dma_start(at(table_v, q), rows[:, :, :]).then_inc(rows_stored, 16)

            def store_out(q):
                sp.wait_ge(post_read, q * POST_USES + POST_USES)
                sp.dma_start(at(out_v, q), outb.rearrange("p (i d) -> p i d", i=NT)).then_inc(out_stored, 16)

            def keep_x(p, h):
                sp.wait_ge(x_summed, p + 1)
                if not (isinstance(p, int) and p < 2):
                    sp.wait_ge(post_read, (p - 2) * POST_USES + POST_MT + 1)
                sp.dma_start(xs[h][:, :, :], xin[:, :, :]).then_inc(xs_ready, 16)

            keep_x(0, 0)
            load_x(1)
            turns(sp, turn)
            store_out(B - 2)
            store(B - 1, 1)
            store_out(B - 1)
            sp.wait_ge(consts, CONSTS)
            sp.dma_start(out[T:T + CAP, :], xd[:, 0:DM]).then_inc(pad_stored, 16)
            sp.wait_ge(counts_ready, B)
            sp.dma_start(ends.rearrange("(e t) -> e t", t=TILES), tile_ends[:, :]).then_inc(ends_stored, 16)
            sp.wait_ge(ends_stored, 16)
            sp.wait_ge(summed, B * N)
            sp.dma_start(big, ends.rearrange("(a n) -> a n", a=1).broadcast_to([P, E * TILES]))\
                .then_inc(ends_back, 16)
            sp.wait_ge(state_ready, B * N)

            def weights(e, r):
                wait(sp, e_o, e - ER + 1)
                a, d = (egu_w[e], edown_w[e]) if isinstance(e, int) else (
                    egu_w[bass.ds(e, 1)].squeeze(0), edown_w[bass.ds(e, 1)].squeeze(0))
                sp.dma_start(ewg[r], a.rearrange("(f p) n -> p f n", p=P)).then_inc(e_weights[r], 16)
                sp.dma_start(ewd[r], d).then_inc(e_weights[r], 16)

            for e in range(ER):
                weights(e, e)
            with sp.Fori(1, E // ER) as it:
                for r in range(ER):
                    weights(it * ER + r, r)
            sp.wait_ge(rows_stored, 16 * B)
            sp.wait_ge(out_stored, 16 * B)
            sp.wait_ge(counts_stored, 16 * B)
            sp.wait_ge(pad_stored, 16)
            sp.wait_ge(e_scattered, 16 * E)

        @block.gpsimd
        def _(pool):
            pool.memset(ident[:, :], 0.0).then_inc(cleared, 1)
            pool.memset(onehot[:, :], 0.0).then_inc(cleared, 1)
            pool.memset(steps_tri[:, :], 1.0).then_inc(cleared, 1)
            pool.memset(w_x[:, :, R:32], 0.0).then_inc(cleared, 1)
            pool.memset(w_dt[:, :], 0.0).then_inc(cleared, 1)
            pool.memset(minus_half[:, :], -0.5).then_inc(cleared, 1)
            pool.wait_ge(cleared, 6)
            pool.affine_select(out=ident[:, :], in_=ident[:, :], compare_op=ALU.not_equal, fill=1.0,
                               base=0, pattern=[[-1, P]], channel_multiplier=1).then_inc(consts, 1)
            for c in range(1, 4):
                if c > 1:
                    pool.wait_ge(consts, c)
                pool.affine_select(out=onehot[:, :], in_=onehot[:, :], compare_op=ALU.not_equal, fill=1.0,
                                   base=-32 * c, pattern=[[-1, 2 * N]], channel_multiplier=1).then_inc(consts, 1)
            pool.affine_select(out=steps_tri[:, :], in_=steps_tri[:, :], compare_op=ALU.is_ge, fill=0.0,
                               base=-3 * P, pattern=[[1, 3 * P + L]], channel_multiplier=-1).then_inc(consts, 1)
            pool.iota(slot[:, :], pattern=[[0, 1]], base=0, channel_multiplier=1,
                      allow_small_or_imprecise_dtypes=True).then_inc(consts, 1)
            pool.iota(slot_pad[:, :], pattern=[[0, 1]], base=T, channel_multiplier=1,
                      allow_small_or_imprecise_dtypes=True).then_inc(consts, 1)
            pool.iota(row_of[:, :], pattern=[[TILES, E]], base=0, channel_multiplier=0,
                      allow_small_or_imprecise_dtypes=True).then_inc(consts, 1)

            def scan_input(b, h, n):
                g = b * N + n
                if n == 0:
                    pool.wait_ge(dt_ready, 2 * b + 2)
                pool.wait_ge(b_copied, g + 1)
                wait(pool, summed, g - HR + 1)
                pool.tensor_tensor(hs[:, n % HR], dtu[h][:, :, :],
                                   b_all[:, n % 2, :].unsqueeze(1).broadcast_to([P, J, L]), ALU.mult)\
                    .then_inc(input_ready, 1)

            def scales(s, which, k):
                wait_apart(pool, s, 3 * k + 2)
                pool.tensor_scalar(rstd[:, which, :].unsqueeze(2), mv[:, which, :, 1:2], EPS, None, ALU.add)\
                    .then_inc(rstd_ready[which], 1)
                pool.wait_ge(rstd_ready[which], 2 * k + 1)
                pool.tensor_tensor(rstd[:, which, :], rstd[:, which, :], minus_half[:, :], ALU.pow)\
                    .then_inc(rstd_ready[which], 1)

            def split_bc(p, h):
                wait_apart(pool, prep_read, PREP_USES * p + PREP_S + 1)
                pool.tensor_copy(parts[h][:, :], xd[:, :]).then_inc(split, 1)
                pool.wait_ge(split, 4 * p + 1)
                pool.tensor_tensor(xd[64:128, :], xd[64:128, :], parts[h][64:128, :], ALU.subtract).then_inc(split, 1)
                wait_apart(pool, split, 4 * p + 2)
                pool.tensor_copy(parts[h][64:128, :], xd[64:128, :]).then_inc(split, 1)
                pool.wait_ge(split, 4 * p + 3)
                pool.tensor_tensor(parts[h][96:128, :], xd[96:128, :], parts[h][96:128, :], ALU.subtract)\
                    .then_inc(split, 1)
                pool.wait_ge(split, 4 * p + 4)

            def step_sizes(p, h):
                pool.wait_ge(soft, 2 * p + 2)
                pool.tensor_tensor(dt[h][:, :, :], dt[h][:, :, :], ab, ALU.add).then_inc(dt_ready, 1)

            def step_inputs(p, h):
                pool.wait_ge(dt_ready, 2 * p + 1)
                pool.tensor_tensor(dtu[h][:, :, :], dt[h][:, :, :], xc[:, :, :], ALU.mult).then_inc(dt_ready, 1)

            def turn(b, h, prep, post, finish):
                for n in range(N):
                    if prep and n == 0:
                        scales(ln0, 0, b + 1)
                    if prep and n == 2:
                        scales(ln1, 1, b + 1)
                    if post and n == LN2_SLOT:
                        scales(ln2, 2, b - 1)
                    if n < N - 2:
                        scan_input(b, h, n + 2)
                    elif prep:
                        scan_input(b + 1, 1 - h, n + 2 - N)
                    if prep and n == SPLIT_SLOT:
                        split_bc(b + 1, 1 - h)
                    if prep and n == STEP_SLOT:
                        step_sizes(b + 1, 1 - h)
                    if prep and n == DTU_SLOT:
                        step_inputs(b + 1, 1 - h)

            scales(ln0, 0, 0)
            scales(ln1, 1, 0)
            split_bc(0, 0)
            step_sizes(0, 0)
            step_inputs(0, 0)
            scan_input(0, 0, 0)
            scan_input(0, 0, 1)
            turns(pool, turn)
            scales(ln2, 2, B - 1)

            pool.wait_ge(split, 4 * B)
            pool.wait_ge(prep_full, B * PREP_USES)
            pool.memset(xd[:, 0:DM], 0.0).then_inc(consts, 1)
            pool.wait_ge(slot_step, 4)
            pool.wait_ge(counts_stored, 16 * B)
            tiles = counts.rearrange("e (t k) -> (e t) k", k=P)
            for e in range(E):
                pool.indirect_dma_start(out=slots3[:, e, :], out_offset=None, in_=tiles,
                                        in_offset=bass.IndirectOffsetOnAxis(ap=idx1[:, e:e + 1], axis=0))\
                    .then_inc(slot_rows, 16)
            pool.wait_ge(rows_stored, 16 * B)
            pool.wait_ge(out_stored, 16 * B)
            pool.wait_ge(pad_stored, 16)

            def gather(e, r):
                pool.wait_ge(ring_ready, e + 1)
                if not (isinstance(e, int) and e < ER):
                    wait_apart(pool, e_res, e - ER + 1)
                pool.indirect_dma_start(out=got[r], out_offset=None, in_=table,
                                        in_offset=bass.IndirectOffsetOnAxis(ap=ring_in[r][:, :], axis=0))\
                    .then_inc(e_gathered[r], 16)

            def scatter(e, r):
                pool.wait_ge(e_res, e + 1)
                if not (isinstance(e, int) and e == 0):
                    wait_apart(pool, e_scattered, e * 16)
                pool.indirect_dma_start(out=out, out_offset=bass.IndirectOffsetOnAxis(ap=ring_out[r][:, :], axis=0),
                                        in_=res_e[r], in_offset=None, compute_op=ALU.add).then_inc(e_scattered, 16)

            AHEAD = 2
            for e in range(AHEAD):
                gather(e, e)
            for e in range(ER):
                gather(e + AHEAD, (e + AHEAD) % ER)
                scatter(e, e)
            with pool.Fori(1, E // ER - 1) as it:
                for r in range(ER):
                    gather(it * ER + r + AHEAD, (r + AHEAD) % ER)
                    scatter(it * ER + r, r)
            for e in range(E - ER, E):
                if e + AHEAD < E:
                    gather(e + AHEAD, (e + AHEAD) % ER)
                scatter(e, e % ER)
            pool.wait_ge(e_scattered, 16 * E)

        @block.scalar
        def _(act):
            act.wait_ge(loaded, 16 * LOADS)
            act.activation(neg_a[:, :, :], neg_a[:, :, :], ACT.Exp).then_inc(made, 1)

            def copy_b(g, n):
                act.wait_ge(b_full, g + 1)
                wait(act, input_ready, g - 1)
                act.copy(b_all[:, n % 2, :], bcbank).then_inc(b_copied, 1)

            def copy_c(g, n):
                act.wait_ge(c_full, g + 1)
                wait(act, readout_ready, g - 1)
                act.copy(c_all[:, n % 2, :], bcbank).then_inc(c_copied, 1)

            def decays(b, h, n, blocks):
                g = b * N + n
                if 0 in blocks:
                    if n == 0:
                        act.wait_ge(dt_ready, 2 * b + 1)
                    wait(act, state_ready, g - 1)
                for j in blocks:
                    i = act.activation(decay[:, n % 2, j, 1:L], dt[h][:, j, 1:L], ACT.Exp, scale=neg_a[:, j, n:n + 1])
                if J - 1 in blocks:
                    i.then_inc(decay_ready, 1)

            def read_xnT(p, f):
                act.wait_ge(prep_full, p * PREP_USES + PREP_T + f + 1)
                act.activation(xnT[:, f, :], prbank, ACT.Identity, bias=b_sb[:, f:f + 1],
                               scale=g_sb[:, f:f + 1]).then_inc(prep_read, 1)

            def read_xp(p, j):
                act.wait_ge(prep_full, p * PREP_USES + PREP_X + j + 1)
                wait(act, dt_ready, 2 * p)
                act.copy(xpad[:, j, PAD:PAD + L], prbank).then_inc(prep_read, 1)

            def read_z(p, h, j):
                act.wait_ge(prep_full, p * PREP_USES + PREP_Z + j + 1)
                wait(act, post_full, (p - 2) * POST_USES + POST_M + 1)
                act.copy(sz[h][:, j, :], prbank).then_inc(prep_read, 1)

            def silus(p, h):
                act.wait_ge(prep_read, p * PREP_USES + PREP_Z + J)
                act.wait_ge(conv_step, (p + 1) * J * TAPS)
                act.activation(xc[:, :, :], xc[:, :, :], ACT.Silu).then_inc(xc_ready, 1)
                act.activation(sz[h][:, :, :], sz[h][:, :, :], ACT.Silu).then_inc(z_ready, 1)

            def read_xd(p):
                act.wait_ge(prep_full, p * PREP_USES + PREP_S + 1)
                wait(act, split, 4 * p)
                act.copy(xd[:, :], prbank).then_inc(prep_read, 1)

            def read_dt(p, h, j):
                act.wait_ge(prep_full, p * PREP_USES + PREP_D + j + 1)
                wait(act, state_ready, (p - 1) * N)
                act.activation(ab[:, j, :], prbank, ACT.Abs, bias=db_sb[:, j:j + 1])
                act.activation(dt[h][:, j, :], prbank, ACT.Relu, bias=db_sb[:, j:j + 1]).then_inc(prep_read, 1)

            def softplus(p):
                act.wait_ge(prep_read, p * PREP_USES + PREP_USES)
                act.activation(ab, ab, ACT.Exp, scale=-1.0).then_inc(soft, 1)
                act.wait_ge(soft, 2 * p + 1)
                act.activation(ab, ab, ACT.Ln, bias=1.0).then_inc(soft, 1)

            def gelu(q):
                act.wait_ge(post_full, q * POST_USES + POST_M + 1)
                wait(act, out_stored, 16 * q)
                act.activation(mT[:, :, :], pobank, ACT.Gelu).then_inc(post_read, 1)

            def glu_gate(q):
                wait(act, post_read, q * POST_USES)
                act.wait_ge(post_full, q * POST_USES + POST_G + 1)
                for f in range(FM):
                    i = act.activation(sg[:, f, :], pobank[:, f, :], ACT.Sigmoid, bias=gb_sb[:, FM + f:FM + f + 1])
                i.then_inc(post_read, 1)

            def read_x2T(q):
                act.wait_ge(post_full, q * POST_USES + POST_XT + 1)
                act.copy(x2T[:, :, :], pobank).then_inc(post_read, 1)

            def router_exp(q):
                act.wait_ge(route, q * ROUTES + 2)
                for i in range(NT):
                    act.activation(pr[:, i, :], lg[:, i, 0:E], ACT.Exp, bias=negmax[:, i:i + 1],
                                   accum_out=esum[:, i:i + 1])
                act.activation(eg.unsqueeze(2), lg[:, :, E:E + 1], ACT.Exp, scale=-1.0).then_inc(exp_ready, 1)

            def read_counts(q, h):
                act.wait_ge(post_full, q * POST_USES + POST_C + 1)
                wait(act, counts_stored, 16 * q)
                act.wait_ge(made, MADE)
                act.activation(cnt[h][:, :], pobank[0:E, 0, :], ACT.Identity, bias=cnt[1 - h][:, L - 1:L])\
                    .then_inc(post_read, 1)
                act.wait_ge(post_read, q * POST_USES + POST_C + 1)
                act.copy(tile_ends[:, bass.ds(q * NT, NT)], cnt[h][:, P - 1:L:P]).then_inc(counts_ready, 1)

            def read_gates(q, k):
                act.wait_ge(post_full, q * POST_USES + (POST_SG, POST_SG2)[k] + 1)
                act.copy(hid[:, 2 * k:2 * k + 2, :], pobank).then_inc(post_read, 1)

            def hid_silu(q):
                act.wait_ge(post_read, q * POST_USES + POST_SG2 + 1)
                act.activation(hid[:, :, :], hid[:, :, :], ACT.Silu).then_inc(hid_ready, 1)

            def prep_at(p, h, at):
                for f in range(FM):
                    if at == T_AT[f]:
                        read_xnT(p, f)
                for j in range(J):
                    if at == X_AT[j]:
                        read_xp(p, j)
                    if at == Z_AT[j]:
                        read_z(p, h, j)
                    if at == D_AT[j]:
                        read_dt(p, h, j)
                if at == SILU_AT:
                    silus(p, h)
                if at == PX_AT[1]:
                    read_xd(p)
                if at == SOFT_AT:
                    softplus(p)

            def post_at(q, h, at):
                if at == M_AT[3]:
                    gelu(q)
                if at == G_AT[1]:
                    glu_gate(q)
                if at == XT_AT:
                    read_x2T(q)
                if at == EXP_AT:
                    router_exp(q)
                if at == SG_AT[1]:
                    read_gates(q, 0)
                if at == C_AT:
                    read_counts(q, h)
                if at == SG_AT[3]:
                    read_gates(q, 1)
                if at == HID_AT:
                    hid_silu(q)

            def turn(b, h, prep, post, finish):
                p, q = b + 1, b - 1

                def others(at):
                    if prep:
                        prep_at(p, 1 - h, at)
                    if post:
                        post_at(q, 1 - h, at)

                for n in range(N):
                    g = b * N + n
                    ahead = (b, h, n + 2) if n < N - 2 else (p, 1 - h, n + 2 - N)
                    more = n < N - 2 or prep
                    if more:
                        decays(*ahead, (0, 1))
                    others((n, 1))
                    if n < N - 3 or prep:
                        copy_b(g + 3, n + 1)
                    if more:
                        decays(*ahead, (2,))
                    others((n, 2))
                    if more:
                        copy_c(g + 2, n)
                        decays(*ahead, (3,))
                    others((n, 3))

            act.wait_ge(made, MADE)
            places = [(n, k) for n in range(N) for k in (1, 2, 3)]
            for at in places:
                prep_at(0, 0, at)
            for n in range(2):
                copy_b(n, n)
                copy_c(n, n)
                decays(0, 0, n, range(J))
            copy_b(2, 2)
            turns(act, turn)
            for at in places:
                post_at(B - 1, 1, at)

            def expert(e, r, first):
                act.wait_ge(e_t, e + 1)
                if not first:
                    act.wait_ge(e_gu, e - 1)
                act.copy(geT[r % 2], ps[:, r % 2, 0:DM].rearrange("p (f n) -> p f n", f=FM)).then_inc(e_tc, 1)
                act.wait_ge(e_gu, e + 1)
                if not first:
                    act.wait_ge(e_hid, e - 1)
                act.activation(act_e[r % 2], ps[:, 2 + r % 2, 0:IE], ACT.Silu).then_inc(e_act, 1)

            for e in range(2):
                expert(e, e, True)
            for e in range(2, ER):
                expert(e, e, False)
            with act.Fori(1, E // ER) as it:
                for r in range(ER):
                    expert(it * ER + r, r, False)

        @block.tensor
        def _(pe):
            def one_row(h, row):
                return pe.matmul(bcbank, onehot[:, row:row + 1].broadcast_to([P, P]), parts[h][:, :],
                                 start=True, stop=True)

            def broadcast_b(g, h, n):
                wait(pe, c_copied, g - 1 if not isinstance(g, int) or g > 2 else g)
                if isinstance(g, int) and g == 3:
                    pe.wait_ge(b_copied, 3)
                one_row(h, n).then_inc(b_full, 1)

            def broadcast_c(g, h, n):
                last = isinstance(g, int) and g == B * N - 1
                pe.wait_ge(b_copied, g + 1 if last else g + 2)
                if last:
                    pe.wait_ge(c_copied, g)
                one_row(h, N + n).then_inc(c_full, 1)

            def start_y(b):
                pe.wait_ge(xc_ready, b + 1)
                wait(pe, y_read, b)
                for j in range(J):
                    pe.matmul(ybank[:, j, :], d_diag[:, j, :], xc[:, j, :], start=True, stop=False)

            def sum_states(g, n, j):
                if j == 0:
                    pe.wait_ge(readout_ready, g + 1)
                i = pe.matmul(ybank[:, j, :], ident[:, :], hs[:, n % HR, j, :], start=False, stop=(n == N - 1))
                if j == J - 1:
                    i.then_inc(summed, 1)

            def use_prep(p, u):
                wait(pe, prep_read, p * PREP_USES + u)

            def turn_xn(p, f):
                pe.wait_ge(ln1, 3 * p + 3)
                use_prep(p, PREP_T + f)
                for i in range(NT):
                    m = pe.transpose(prbank[:, i * P:(i + 1) * P], xn[:, i, f * P:(f + 1) * P], ident[:, :])
                m.then_inc(prep_full, 1)

            def project_in(p, u, col):
                pe.wait_ge(prep_read, p * PREP_USES + PREP_T + FM)
                use_prep(p, u)
                for f in range(FM):
                    m = pe.matmul(prbank, w_in[:, f, col * P:(col + 1) * P], xnT[:, f, :],
                                  start=(f == 0), stop=(f == FM - 1))
                m.then_inc(prep_full, 1)

            def project_x(p, half):
                if half == 0:
                    pe.wait_ge(xc_ready, p + 1)
                    use_prep(p, PREP_S)
                for j in (2 * half, 2 * half + 1):
                    m = pe.matmul(prbank, w_x[:, j, :], xc[:, j, :], start=(j == 0), stop=(j == J - 1))
                if half == 1:
                    m.then_inc(prep_full, 1)

            def project_dt(p, j):
                if j == 0:
                    pe.wait_ge(prep_read, p * PREP_USES + PREP_S + 1)
                use_prep(p, PREP_D + j)
                pe.matmul(prbank, w_dt[:, j * P:(j + 1) * P], xd[0:2 * R, :], start=True, stop=True)\
                    .then_inc(prep_full, 1)

            def use_post(q, u):
                wait(pe, post_read, q * POST_USES + u)

            def project_out(q, h, c):
                f, half = c // 2, c % 2
                if c == 0:
                    pe.wait_ge(y_read, q + 1)
                    use_post(q, POST_M)
                for j in (2 * half, 2 * half + 1):
                    m = pe.matmul(pobank[:, f, :], w_out[:, j, f * P:(f + 1) * P], sz[h][:, j, :],
                                  start=(j == 0), stop=(j == J - 1))
                if c == 3:
                    m.then_inc(post_full, 1)

            def project_glu(q, u, half, f):
                if f == 0:
                    use_post(q, u)
                for k in range(FM):
                    col = (half * FM + f) * P
                    m = pe.matmul(pobank[:, f, :], w_glu[:, k, col:col + P], mT[:, k, :],
                                  start=(k == 0), stop=(k == FM - 1))
                if f == FM - 1:
                    m.then_inc(post_full, 1)

            def turn_m(q):
                use_post(q, POST_MT)
                for i in range(NT):
                    for f in range(FM):
                        m = pe.transpose(po_tok[:, i, f * P:(f + 1) * P], sg[:, f, i * P:(i + 1) * P], ident[:, :])
                m.then_inc(post_full, 1)

            def turn_x2(q):
                pe.wait_ge(ln2, 3 * q + 3)
                use_post(q, POST_XT)
                for f in range(FM):
                    for i in range(NT):
                        m = pe.transpose(pobank[:, f, i * P:(i + 1) * P], rows[:, i, f * P:(f + 1) * P], ident[:, :])
                m.then_inc(post_full, 1)

            def logits(q):
                use_post(q, POST_R)
                for i in range(NT):
                    for f in range(FM):
                        m = pe.matmul(pobank[:, 0, i * P:i * P + E + 1], x2T[:, f, i * P:(i + 1) * P], w_r[:, f, :],
                                      start=(f == 0), stop=(f == FM - 1))
                m.then_inc(post_full, 1)

            def count(q):
                pe.wait_ge(route, q * ROUTES + MASK_STEP)
                use_post(q, POST_C)
                for i in range(NT):
                    at = (NT - 1 - i) * P
                    m = pe.matmul(pobank[0:E, 0, :], maskb[:, i, :], steps_tri[:, at:at + L],
                                  start=(i == 0), stop=(i == NT - 1))
                m.then_inc(post_full, 1)

            def shared_up(q, u, block, k):
                if k == 0:
                    use_post(q, u)
                for f in range(FM):
                    m = pe.matmul(pobank[:, k, :], w_sgu[:, f, block * P:(block + 1) * P], x2T[:, f, :],
                                  start=(f == 0), stop=(f == FM - 1))
                if k == 1:
                    m.then_inc(post_full, 1)

            def shared_down(q, i):
                if i == 0:
                    use_post(q, POST_DN)
                for k in range(KS):
                    m = pe.matmul(po_tok[:, i, :], hid[:, k, i * P:(i + 1) * P], w_sd[:, k, :],
                                  start=(k == 0), stop=(k == KS - 1))
                if i == NT - 1:
                    m.then_inc(post_full, 1)

            def prep_at(p, at):
                for f in range(FM):
                    if at == T_AT[f]:
                        turn_xn(p, f)
                for j in range(J):
                    if at == X_AT[j]:
                        project_in(p, PREP_X + j, j)
                    if at == Z_AT[j]:
                        project_in(p, PREP_Z + j, J + j)
                    if at == D_AT[j]:
                        project_dt(p, j)
                for half in range(2):
                    if at == PX_AT[half]:
                        project_x(p, half)

            def post_at(q, h, at):
                for c in range(4):
                    if at == M_AT[c]:
                        project_out(q, h, c)
                for f in range(FM):
                    if at == G_AT[f]:
                        project_glu(q, POST_G, 1, f)
                    if at == V_AT[f]:
                        project_glu(q, POST_V, 0, f)
                if at == MT_AT:
                    turn_m(q)
                if at == XT_AT:
                    turn_x2(q)
                if at == R_AT:
                    logits(q)
                if at == C_AT:
                    count(q)
                for k in range(KS):
                    if at == SG_AT[k]:
                        shared_up(q, (POST_SG, POST_SG2)[k // 2], k, k % 2)
                    if at == SU_AT[k]:
                        shared_up(q, (POST_SU, POST_SU2)[k // 2], KS + k, k % 2)
                if at == DN_AT[0]:
                    shared_down(q, 0)

            def finish_at(q, at):
                for i in range(1, NT):
                    if at == DN_AT[i]:
                        shared_down(q, i)

            def turn(b, h, prep, post, finish):
                p, q = b + 1, b - 1

                def others(at):
                    if finish:
                        finish_at(q - 1, at)
                    if prep:
                        prep_at(p, at)
                    if post:
                        post_at(q, 1 - h, at)

                for n in range(N):
                    g = b * N + n
                    others((n, 1))
                    if n == 0:
                        start_y(b)
                    sum_states(g, n, 0)
                    if n < N - 3:
                        broadcast_b(g + 3, h, n + 3)
                    elif prep:
                        if n == N - 3:
                            pe.wait_ge(split, 4 * p + 4)
                        broadcast_b(g + 3, 1 - h, n + 3 - N)
                    sum_states(g, n, 1)
                    others((n, 2))
                    sum_states(g, n, 2)
                    if n < N - 2:
                        broadcast_c(g + 2, h, n + 2)
                    elif prep:
                        broadcast_c(g + 2, 1 - h, n + 2 - N)
                    sum_states(g, n, 3)
                    others((n, 3))

            pe.wait_ge(loaded, 16 * LOADS)
            pe.wait_ge(consts, 8)
            pe.wait_ge(made, MADE)
            places = [(n, k) for n in range(N) for k in (1, 2, 3)]
            for at in places:
                prep_at(0, at)
            pe.wait_ge(split, 4)
            for n in range(2):
                broadcast_b(n, 0, n)
                pe.wait_ge(b_copied, n + 1)
                one_row(0, N + n).then_inc(c_full, 1)
            pe.wait_ge(c_copied, 2)
            broadcast_b(2, 0, 2)
            turns(pe, turn)
            for at in places:
                finish_at(B - 2, at)
                post_at(B - 1, 1, at)
            for at in places:
                finish_at(B - 1, at)

            def expert(e, r, first):
                pe.wait_ge(e_gathered[r], (e // ER + 1) * 16 if isinstance(e, int) else e_turn(e, r))
                if not first:
                    pe.wait_ge(e_tc, e - 1)
                for f in range(FM):
                    m = pe.transpose(ps[:, r % 2, f * P:(f + 1) * P], got[r][:, f * P:(f + 1) * P], ident[:, :])
                m.then_inc(e_t, 1)
                pe.wait_ge(e_weights[r], (e // ER + 1) * 32 if isinstance(e, int) else e_turn(e, r) * 2)
                pe.wait_ge(e_tc, e + 1)
                if not first:
                    pe.wait_ge(e_hid, e - 1)
                for half in range(2):
                    for f in range(FM):
                        m = pe.matmul(ps[:, 2 + r % 2, half * IE:(half + 1) * IE],
                                      ewg[r][:, f, half * IE:(half + 1) * IE], geT[r % 2][:, f, :],
                                      start=(f == 0), stop=(f == FM - 1))
                m.then_inc(e_gu, 1)
                pe.wait_ge(e_hid, e + 1)
                if not first:
                    pe.wait_ge(e_res, e - 1)
                pe.matmul(ps[:, 4 + r % 2, 0:DM], hid_e[r % 2], ewd[r], start=True, stop=True).then_inc(e_o, 1)

            for e in range(ER):
                expert(e, e, e < 2)
            with pe.Fori(1, E // ER) as it:
                def e_turn(e, r):
                    return it * 16 + 16
                for r in range(ER):
                    expert(it * ER + r, r, False)

        @block.vector
        def _(dve):
            for k, t in enumerate((decay[:, :, :, 0:1], xpad[:, :, 0:PAD], cnt[1][:, L - 1:L])):
                dve.memset(t, 0.0).then_inc(made, 1)
            dve.wait_ge(loaded, 16 * LOADS)
            dve.wait_ge(made, 4)
            dve.tensor_scalar(neg_a[:, :, :], neg_a[:, :, :], -1.0, None, ALU.mult).then_inc(made, 1)
            dve.wait_ge(consts, 8)
            for j in range(J):
                dve.tensor_scalar(d_diag[:, j, :], ident[:, :], d_sb[:, j:j + 1], None, ALU.mult).then_inc(made, 1)

            def moments(s, which, k, src):
                for i in range(NT):
                    m = dve.bn_stats(stats[:, which, i, :], src[:, i, :])
                m.then_inc(s, 1)
                wait_apart(dve, s, 3 * k + 1)
                for i in range(NT):
                    m = dve.bn_aggr(mv[:, which, i, :], stats[:, which, i, :])
                m.then_inc(s, 1)

            def normalise(s, which, k, src, dst):
                dve.wait_ge(rstd_ready[which], 2 * k + 2)
                for i in range(NT):
                    m = dve.tensor_scalar(dst[:, i, 0:DM], src[:, i, :], mv[:, which, i, 0:1],
                                          rstd[:, which, i:i + 1], ALU.subtract, ALU.mult)
                m.then_inc(s, 1)

            def moments_x(p):
                dve.wait_ge(x_loaded, 16 * p + 16)
                moments(ln0, 0, p, xin)

            def norm_x(p):
                wait(dve, prep_full, (p - 1) * PREP_USES + PREP_T + FM)
                wait(dve, post_read, (p - 2) * POST_USES)
                normalise(ln0, 0, p, xin, xn)
                dve.wait_ge(ln0, 3 * p + 3)
                dve.tensor_tensor(xin[:, :, :], xin[:, :, :], xn[:, :, :], ALU.add).then_inc(x_summed, 1)
                moments(ln1, 1, p, xn)

            def norm_again(p):
                dve.wait_ge(x_summed, p + 1)
                normalise(ln1, 1, p, xn, xn)

            def conv(p, j):
                dve.wait_ge(prep_read, p * PREP_USES + PREP_X + j + 1)
                if j == 0:
                    wait(dve, summed, (p - 1) * N + 1)
                dve.tensor_scalar(xc[:, j, :], xpad[:, j, 0:L], cw_sb[:, j, 0:1], cb_sb[:, j:j + 1],
                                  ALU.mult, ALU.add).then_inc(conv_step, 1)
                for k in range(1, TAPS):
                    dve.wait_ge(conv_step, (p * J + j) * TAPS + k)
                    dve.scalar_tensor_tensor(xc[:, j, :], xpad[:, j, k:k + L], cw_sb[:, j, k:k + 1], xc[:, j, :],
                                             ALU.mult, ALU.add).then_inc(conv_step, 1)

            def gate_y(q, h):
                dve.wait_ge(summed, (q + 1) * N)
                dve.wait_ge(z_ready, q + 1)
                dve.tensor_tensor(sz[h][:, :, :], ybank, sz[h][:, :, :], ALU.mult).then_inc(y_read, 1)

            def glu(q):
                dve.wait_ge(post_full, q * POST_USES + POST_V + 1)
                dve.wait_ge(post_read, q * POST_USES + POST_G + 1)
                for f in range(FM):
                    i = dve.scalar_tensor_tensor(sg[:, f, :], pobank[:, f, :], gb_sb[:, f:f + 1], sg[:, f, :],
                                                 ALU.add, ALU.mult)
                i.then_inc(post_read, 1)

            def add_m(q, h):
                dve.wait_ge(post_full, q * POST_USES + POST_MT + 1)
                dve.wait_ge(xs_ready, 16 * q + 16)
                dve.tensor_tensor(x1[:, :, :], po_tok, xs[h][:, :, :], ALU.add).then_inc(post_read, 1)

            def moments_x1(q):
                dve.wait_ge(post_read, q * POST_USES + POST_MT + 1)
                moments(ln2, 2, q, x1)

            def norm_x1(q):
                wait(dve, rows_stored, 16 * q)
                normalise(ln2, 2, q, x1, rows)

            def read_logits(q):
                dve.wait_ge(post_full, q * POST_USES + POST_R + 1)
                dve.tensor_copy(lg[:, :, :], pobank[:, 0, :].rearrange("p (i c) -> p i c", i=NT)[:, :, 0:E + 1])\
                    .then_inc(post_read, 1)
                dve.wait_ge(post_read, q * POST_USES + POST_R + 1)
                dve.tensor_reduce(negmax, lg[:, :, 0:E], AX.X, ALU.max, negate=True).then_inc(route, 2)

            def choose(q):
                at = [q * ROUTES + 2]

                def link(i):
                    i.then_inc(route, 1)
                    at[0] = at[0] + 1
                    wait_apart(dve, route, at[0])

                def wide(t, w):
                    return t.unsqueeze(2).broadcast_to([P, NT, w])

                dve.wait_ge(exp_ready, q + 1)
                dve.reciprocal(rsum, esum)
                link(dve.tensor_scalar(gate_s, eg, 1.0, None, ALU.add))
                dve.reciprocal(gate_s, gate_s)
                link(dve.tensor_tensor(pr[:, :, :], pr[:, :, :], wide(rsum, E), ALU.mult))
                for i in range(NT):
                    k = dve.max(top[:, i, :], pr[:, i, :])
                link(k)
                for i in range(NT):
                    dve.match_replace(rep[:, i, :], top[:, i, :], pr[:, i, :], -1.0)
                link(dve.tensor_reduce(s8, top[:, :, :], AX.X, ALU.add))
                dve.reciprocal(s8, s8)
                link(dve.tensor_tensor(rep[:, :, :], rep[:, :, :], pr[:, :, :], ALU.not_equal))
                link(dve.tensor_copy(maskb[:, :, :], rep[:, :, :]))
                link(dve.tensor_tensor(pr[:, :, :], pr[:, :, :], rep[:, :, :], ALU.mult))
                dve.tensor_tensor(rows[:, :, DM:ROW], pr[:, :, :], wide(s8, E), ALU.mult).then_inc(route, 1)

            def mul_up(q, k):
                dve.wait_ge(post_full, q * POST_USES + POST_SU + k + 1)
                if k == 0:
                    dve.wait_ge(hid_ready, q + 1)
                dve.tensor_tensor(hid[:, 2 * k:2 * k + 2, :], pobank, hid[:, 2 * k:2 * k + 2, :], ALU.mult)\
                    .then_inc(post_read, 1)

            def add_shared(q):
                dve.wait_ge(post_full, q * POST_USES + POST_DN + 1)
                for i in range(NT):
                    k = dve.scalar_tensor_tensor(outb[:, i * DM:(i + 1) * DM], po_tok[:, i, :], gate_s[:, i:i + 1],
                                                 x1[:, i, :],
                                                 ALU.mult, ALU.add)
                k.then_inc(post_read, 1)

            def in_step(q, h, n):
                if n == ADD_SLOT:
                    add_m(q, h)
                if n == LN2_SLOT:
                    norm_x1(q)
            def after_step(q, h, n):
                if n == UP_SLOTS[0]:
                    mul_up(q, 0)
                if n == UP_SLOTS[1]:
                    mul_up(q, 1)
                if n == GLU_SLOT:
                    glu(q)
                if n == ADD_SLOT:
                    moments_x1(q)
                if n == LOGIT_SLOT:
                    read_logits(q)
                if n == CHOOSE_SLOT:
                    choose(q)

            def turn(b, h, prep, post, finish):
                p, q = b + 1, b - 1
                for n in range(N):
                    g = b * N + n
                    dve.wait_ge(decay_ready, g + 1)
                    dve.wait_ge(input_ready, g + 1)
                    dve.tensor_tensor_scan(hs[:, n % HR].rearrange("p j l -> p (j l)"),
                                           decay[:, n % 2].rearrange("p j l -> p (j l)"),
                                           hs[:, n % HR].rearrange("p j l -> p (j l)"), 0.0, ALU.mult, ALU.add)\
                        .then_inc(state_ready, 1)
                    if post:
                        if n == 0:
                            gate_y(q, 1 - h)
                        in_step(q, 1 - h, n)
                    dve.wait_ge(state_ready, g + 1)
                    dve.wait_ge(c_copied, g + 1)
                    dve.tensor_tensor(hs[:, n % HR], hs[:, n % HR],
                                      c_all[:, n % 2, :].unsqueeze(1).broadcast_to([P, J, L]), ALU.mult)\
                        .then_inc(readout_ready, 1)
                    if finish and n == END_SLOT:
                        add_shared(q - 1)
                    if prep:
                        if n == 1:
                            norm_x(p)
                        if n == 2:
                            norm_again(p)
                        for j in range(J):
                            if n == CONV_SLOTS[j]:
                                conv(p, j)
                    if post:
                        after_step(q, 1 - h, n)
                    if n == N - 1 and not (isinstance(b, int) and b + 2 >= B):
                        moments_x(p + 1)

            moments_x(0)
            norm_x(0)
            norm_again(0)
            for j in range(J):
                conv(0, j)
            moments_x(1)
            turns(dve, turn)
            add_shared(B - 2)
            gate_y(B - 1, 1)
            for n in range(N):
                in_step(B - 1, 1, n)
                after_step(B - 1, 1, n)
            add_shared(B - 1)

            dve.wait_ge(ends_back, 16)
            dve.wait_ge(consts, 8)
            dve.tensor_scalar(big, big, slot[:, 0:1], None, ALU.is_le).then_inc(slot_step, 1)
            dve.wait_ge(slot_step, 1)
            dve.tensor_reduce(tau, slots3, AX.X, ALU.add).then_inc(slot_step, 1)
            dve.wait_ge(slot_step, 2)
            dve.scalar_tensor_tensor(loc, tau, float(TILES - 1), row_of[:, :], ALU.min, ALU.add)\
                .then_inc(slot_step, 1)
            dve.wait_ge(slot_step, 3)
            dve.tensor_copy(idx1, loc).then_inc(slot_step, 1)
            dve.wait_ge(slot_rows, 16 * E)
            dve.tensor_scalar(big, big, slot[:, 0:1], None, ALU.is_le).then_inc(slot_step, 1)
            dve.wait_ge(slot_step, 5)
            dve.tensor_reduce(loc, slots3, AX.X, ALU.add).then_inc(slot_step, 1)
            dve.wait_ge(slot_step, 6)
            dve.scalar_tensor_tensor(loc, tau, float(P), loc, ALU.mult, ALU.add).then_inc(slot_step, 1)
            dve.wait_ge(slot_step, 7)
            dve.tensor_scalar(idx_in, loc, float(T - 1), None, ALU.min).then_inc(slot_step, 1)
            dve.tensor_scalar(idx_out, loc, slot_pad[:, 0:1], None, ALU.min).then_inc(slot_step, 1)
            dve.wait_ge(slot_step, 9)

            def indices(e, r):
                wait(dve, e_scattered, (e - ER + 1) * 16)
                dve.tensor_copy(ring_out[r][:, :], idx_out[:, bass.ds(e, 1)])
                dve.tensor_copy(ring_in[r][:, :], idx_in[:, bass.ds(e, 1)]).then_inc(ring_ready, 1)

            def expert(e, r, first):
                dve.wait_ge(e_act, e + 1)
                if not first:
                    dve.wait_ge(e_o, e - 1)
                dve.tensor_tensor(hid_e[r % 2], ps[:, 2 + r % 2, IE:2 * IE], act_e[r % 2], ALU.mult).then_inc(e_hid, 1)
                dve.wait_ge(e_o, e + 1)
                dve.wait_ge(ring_ready, e + 1)
                dve.tensor_scalar(res_e[r], ps[:, 4 + r % 2, 0:DM], got[r][:, bass.ds(e + DM, 1)], None, ALU.mult)\
                    .then_inc(e_res, 1)

            AHEAD = 2
            for e in range(AHEAD):
                indices(e, e)
            for e in range(ER):
                indices(e + AHEAD, (e + AHEAD) % ER)
                expert(e, e, e < 2)
            with dve.Fori(1, E // ER - 1) as it:
                for r in range(ER):
                    indices(it * ER + r + AHEAD, (r + AHEAD) % ER)
                    expert(it * ER + r, r, False)
            for e in range(E - ER, E):
                if e + AHEAD < E:
                    indices(e + AHEAD, (e + AHEAD) % ER)
                expert(e, e % ER, False)


ROUTES, MASK_STEP = 10, 8
CONSTS, MADE = 9, 9
LOADS = 14
T_AT = (3, 1), (3, 3)
X_AT = (4, 1), (4, 3), (5, 2), (6, 1)
CONV_SLOTS = 5, 6, 6, 7
Z_AT = (6, 3), (7, 1), (7, 3), (8, 1)
SILU_AT = (8, 3)
PX_AT = (9, 2), (9, 3)
D_AT = (10, 1), (10, 3), (11, 1), (11, 3)
SPLIT_SLOT = 11
SOFT_AT = (12, 2)
STEP_SLOT = 12
DTU_SLOT = 13
M_AT = (1, 3), (2, 1), (2, 2), (2, 3)
G_AT = (3, 2), (3, 3)
V_AT = (4, 2), (5, 1)
GLU_SLOT = 5
MT_AT = (6, 2)
ADD_SLOT = 7
LN2_SLOT = 8
XT_AT = (8, 2)
R_AT = (9, 1)
LOGIT_SLOT = 9
EXP_AT = (9, 2)
CHOOSE_SLOT = 10
SG_AT = (10, 1), (10, 2), (11, 2), (11, 3)
C_AT = (12, 1)
HID_AT = (13, 1)
SU_AT = (12, 3), (13, 1), (14, 1), (14, 3)
UP_SLOTS = 13, 15
DN_AT = (15, 3), (0, 1), (0, 1), (0, 3)
END_SLOT = 1


def kernel(**inputs):
    import concourse.bacc as bacc
    import numpy as np
    from concourse.bass_utils import run_bass_kernel_spmd as run

    nc = bacc.Bacc("TRN2", target_bir_lowering=False, num_devices=1)
    a, f = "L0_attn_", "L0_ffn_"
    vectors = np.concatenate([np.asarray(inputs[a + v]).reshape(-1, P).T for v in (
        "ln_g", "ln_b", "conv_b", "dt_proj_b", "D", "glu_b")], axis=1)
    laid = {
        "x": inputs[a + "x"], "vectors": vectors,
        "in_wT": np.asarray(inputs[a + "in_proj_w"]).T, "conv_w": inputs[a + "conv_w"],
        "x_wT": np.asarray(inputs[a + "x_proj_w"]).T, "dt_wT": np.asarray(inputs[a + "dt_proj_w"]).T,
        "a_log": inputs[a + "A_log"], "out_wT": np.asarray(inputs[a + "out_proj_w"]).T,
        "glu_wT": np.asarray(inputs[a + "glu_w"]).T,
        "router_w": np.concatenate([inputs[f + "gate_w"], inputs[f + "shared_gate_w"]], axis=1),
        "sgu_w": inputs[f + "shared_gate_up_w"], "sdown_w": inputs[f + "shared_down_w"],
        "egu_w": inputs[f + "expert_gate_up_w"], "edown_w": inputs[f + "expert_down_w"],
    }
    arrays, args = {}, []
    for name, v in laid.items():
        v = np.ascontiguousarray(v)
        arrays[name] = v
        args.append(nc.dram_tensor(name, v.shape, mybir.dt.from_np(v.dtype), kind="ExternalInput").ap())
    args.append(nc.dram_tensor("out", [T + CAP, DM], F32, kind="ExternalOutput").ap())
    args.append(nc.dram_tensor("counts", [E, T], F32, kind="Internal").ap())
    args.append(nc.dram_tensor("table", [T, ROW], F32, kind="Internal").ap())
    args.append(nc.dram_tensor("ends", [E * TILES], F32, kind="Internal").ap())
    mamba_moe(nc, *args)
    r = run(nc, [arrays], core_ids=[0])
    return r.results[0]["out"][0:T].reshape(B, L, DM)
```

```python
from contextlib import ExitStack

import concourse.bass as bass
from concourse import mybir

F32 = mybir.dt.float32
BF16 = mybir.dt.bfloat16
I32 = mybir.dt.int32
ACT = mybir.ActivationFunctionType
ALU = mybir.AluOpType
AX = mybir.AxisListType

P = 128
B, L, DM = 32, 512, 256
T = B * L
NT = L // P
FM = DM // P
DI = 2 * DM
J = DI // P
N = 16
R = 16
TAPS = 4
PAD = TAPS - 1
E, CAP, TOPK = 64, 128, 8
IS = 512
KS = IS // P
IE = 128
ROW = DM + E
TILES = T // P
EPS = 1e-5
HR = 4
PREP_T, PREP_X, PREP_Z, PREP_S, PREP_D, PREP_USES = 0, 2, 6, 10, 11, 15
(POST_M, POST_G, POST_V, POST_MT, POST_XT, POST_R, POST_SG,
 POST_SG2, POST_C, POST_SU, POST_SU2, POST_DN, POST_USES) = range(13)


def mamba_moe(nc, x, vectors, in_wT, conv_w, x_wT, dt_wT, a_log, out_wT, glu_wT, router_w, sgu_w, sdown_w, egu_w, edown_w, out, counts, table, ends):
    ctx = ExitStack()
    with ctx:
        def sb(name, shape, dt=F32):
            return ctx.enter_context(nc.sbuf_tensor(name, shape, dt))

        def sem(name):
            return ctx.enter_context(nc.semaphore(name))

        ident = sb("ident", [P, P])
        onehot = sb("onehot", [P, 2 * N], BF16)
        steps_tri = sb("steps_tri", [P, 3 * P + L], BF16)
        slot = sb("slot", [P, 1])
        slot_pad = sb("slot_pad", [P, 1])
        row_of = sb("row_of", [P, E])
        d_diag = sb("d_diag", [P, J, P])
        neg_a = sb("neg_a", [P, J, N])
        vecs = sb("vecs", [P, 20])
        g_sb, b_sb = vecs[:, 0:2], vecs[:, 2:4]
        cb_sb, db_sb, d_sb = vecs[:, 4:8], vecs[:, 8:12], vecs[:, 12:16]
        gb_sb = vecs[:, 16:20]
        cw_sb = sb("cw_sb", [P, J, TAPS])
        w_in = sb("w_in", [P, FM, 2 * DI])
        w_x = sb("w_x", [P, J, P])
        w_dt = sb("w_dt", [2 * R, DI])
        w_out = sb("w_out", [P, J, DM])
        w_glu = sb("w_glu", [P, FM, 2 * DM])
        w_r = sb("w_r", [P, FM, E + 1])
        w_sgu = sb("w_sgu", [P, FM, 2 * IS])
        w_sd = sb("w_sd", [P, KS, DM])

        decay = sb("decay", [P, 2, J, L])
        hs = sb("hs", [P, HR, J, L])
        b_all = sb("b_all", [P, 2, L])
        c_all = sb("c_all", [P, 2, L])
        xin = sb("xin", [P, NT, DM])
        xn = sb("xn", [P, NT, DM])
        xnT = sb("xnT", [P, FM, L])
        xpad = sb("xpad", [P, J, PAD + L])
        xc = sb("xc", [P, J, L])
        xd = sb("xd", [P, L])
        parts = [sb(f"parts{h}", [P, L], BF16) for h in range(2)]
        sz = [sb(f"sz{h}", [P, J, L]) for h in range(2)]
        dt = [sb(f"dt{h}", [P, J, L]) for h in range(2)]
        dtu = [sb(f"dtu{h}", [P, J, L]) for h in range(2)]
        stats = sb("stats", [P, 3, NT, 6])
        mv = sb("mv", [P, 3, NT, 2])
        rstd = sb("rstd", [P, 3, NT])
        minus_half = sb("minus_half", [P, NT])
        xs = [sb(f"xs{h}", [P, NT, DM]) for h in range(2)]
        hid = sb("hid", [P, J, L])
        mT = sb("mT", [P, FM, L])
        rows = sb("rows", [P, NT, ROW])
        lg = sb("lg", [P, NT, E + 1])
        pr = sb("pr", [P, NT, E])
        rep = sb("rep", [P, NT, E])
        top = sb("top", [P, NT, TOPK])
        maskb = sb("maskb", [P, NT, E], BF16)
        small = sb("small", [P, 6, NT])
        cnt = [sb(f"cnt{h}", [E, L]) for h in range(2)]
        tile_ends = sb("tile_ends", [E, TILES])
        ab = xpad[:, :, PAD:PAD + L]
        sg = xn[:, :, :].rearrange("p a b -> p (a b)").rearrange("p (f l) -> p f l", f=FM)
        x2T, x1 = mT, xn
        outb = mT[:, :, :].rearrange("p f l -> p (f l)")
        negmax, esum, rsum, s8, eg, gate_s = (small[:, i, :] for i in range(6))
        tau, first, loc = (dt[0][:, 0, i * E:(i + 1) * E] for i in range(3))
        idx_tile = dt[0][:, 1, 0:E].bitcast(I32)
        ER = 4
        IR = 8
        ring_tile, ring_in, ring_out = (
            [dt[0][:, 2, u * IR + i:u * IR + i + 1].bitcast(I32) for i in range(IR)] for u in range(3))
        token = [dt[0][:, 2, 3 * IR + i:3 * IR + i + 1] for i in range(2)]
        big = hs[:, :, :, :].rearrange("p a j l -> p (a j l)")
        ends3 = big.rearrange("p (e t) -> p e t", e=E)

        def pieces(buffer, start, count, width):
            whole = buffer[:, :, :].rearrange("p j l -> p (j l)")
            return [whole[:, start + i * width:start + (i + 1) * width] for i in range(count)]

        flat = decay[:, :, :, :].rearrange("p a j l -> p (a j l)")
        ewg = [flat[:, i * 768:i * 768 + 512].rearrange("p (f n) -> p f n", f=FM) for i in range(ER)]
        ewd = [flat[:, i * 768 + 512:i * 768 + 768] for i in range(ER)]
        got = pieces(dt[1], 0, ER, ROW)
        geT = [t.rearrange("p (f n) -> p f n", f=FM) for t in pieces(dt[1], ER * ROW, 2, DM)]
        tile_counts = pieces(dtu[0], 0, IR, P)
        res_e = pieces(sz[0], 0, ER, DM)
        act_e = pieces(sz[0], ER * DM, 2, IE)
        hid_e = pieces(sz[0], ER * DM + 2 * IE, 2, IE)

        ps = ctx.enter_context(nc.psum_tensor("ps", [P, 8, L], F32))
        ybank = ps[:, 0:4, :]
        bcbank = ps[:, 4, :]
        prbank = ps[:, 5, :]
        pobank = ps[:, 6:8, :]
        po_tok = pobank.rearrange("p a b -> p (a b)").rearrange("p (i d) -> p i d", i=NT)

        loaded, post_loaded = sem("loaded"), sem("post_loaded")
        consts = sem("consts")
        cleared = sem("cleared")
        made = sem("made")
        passed = sem("passed")
        x_loaded = sem("x_loaded")
        ln0, ln1, ln2 = sem("ln0"), sem("ln1"), sem("ln2")
        rstd_ready = [sem(f"rstd_ready{i}") for i in range(3)]
        prep_full, prep_read = sem("prep_full"), sem("prep_read")
        post_full, post_read = sem("post_full"), sem("post_read")
        conv_step = sem("conv_step")
        xc_ready = sem("xc_ready")
        z_ready = sem("z_ready")
        split = sem("split")
        soft = sem("soft")
        dt_ready = sem("dt_ready")
        x_summed, xs_ready = sem("x_summed"), sem("xs_ready")
        b_full, b_copied = sem("b_full"), sem("b_copied")
        c_full, c_copied = sem("c_full"), sem("c_copied")
        decay_ready = sem("decay_ready")
        input_ready = sem("input_ready")
        state_ready = sem("state_ready")
        readout_ready = sem("readout_ready")
        summed = sem("summed")
        y_read = sem("y_read")
        route = sem("route")
        exp_ready = sem("exp_ready")
        hid_ready = sem("hid_ready")
        counts_ready = sem("counts_ready")
        rows_stored, out_stored, counts_stored = sem("rows_stored"), sem("out_stored"), sem("counts_stored")
        ends_stored = sem("ends_stored")
        ends_back = [sem(f"ends_back{c}") for c in range(CHUNKS)]
        pad_stored = sem("pad_stored")
        slot_step = sem("slot_step")
        tile_ready = sem("tile_ready")
        find_step = sem("find_step")
        t_gathered = [sem(f"t_gathered{i}") for i in range(IR)]
        ring_ready, e_scattered = sem("ring_ready"), sem("e_scattered")
        e_gathered = [sem(f"e_gathered{i}") for i in range(ER)]
        e_weights = [sem(f"e_weights{i}") for i in range(ER)]
        e_t, e_tc, e_gu, e_act, e_hid, e_o, e_res = (
            sem(n) for n in ("e_t", "e_tc", "e_gu", "e_act", "e_hid", "e_o", "e_res"))

        x_v = x.rearrange("b (i p) d -> b p i d", p=P)
        out_v = out[0:T, :].rearrange("(b i p) d -> b p i d", p=P, i=NT)
        table_v = table.rearrange("(b i p) d -> b p i d", p=P, i=NT)
        counts_v = counts.rearrange("e (b l) -> b e l", l=L)

        block = ctx.enter_context(nc.Block())

        def turns(eng, turn):
            turn(0, 0, True, False, False)
            turn(1, 1, True, True, False)
            with eng.Fori(1, B // 2 - 1) as it:
                turn(it * 2, 0, True, True, True)
                turn(it * 2 + 1, 1, True, True, True)
            turn(B - 2, 0, True, True, True)
            turn(B - 1, 1, False, True, True)

        def wait(eng, s, value):
            if not (isinstance(value, int) and value <= 0):
                eng.wait_ge(s, value)

        def wait_apart(eng, s, value):
            eng.wait_ge(s, value)
            if not isinstance(value, int):
                eng.sem_inc(passed, 1)

        @block.sync
        def _(sp):
            def load_x(b):
                sp.wait_ge(xs_ready, 16 * b)
                sp.dma_start(xin[:, :, :], at(x_v, b)).then_inc(x_loaded, 16)

            sp.dma_start(xin[:, :, :], x_v[0]).then_inc(x_loaded, 16)
            sp.wait_ge(cleared, 6)
            for dst, src in (
                (vecs[:, :], vectors),
                (w_in[:, :, :], in_wT.rearrange("(f p) n -> p f n", p=P)),
                (cw_sb[:, :, :], conv_w.rearrange("(j p) o k -> p j (o k)", p=P)),
                (w_x[:, :, 0:R], x_wT[:, 0:R].rearrange("(j p) n -> p j n", p=P)),
                (w_x[:, :, 32:64], x_wT[:, R:R + 2 * N].rearrange("(j p) n -> p j n", p=P)),
                (w_x[:, :, 64:96], x_wT[:, R:R + 2 * N].rearrange("(j p) n -> p j n", p=P)),
                (w_x[:, :, 96:128], x_wT[:, R:R + 2 * N].rearrange("(j p) n -> p j n", p=P)),
                (w_dt[0:R, :], dt_wT),
                (neg_a[:, :, :], a_log.rearrange("(j p) n -> p j n", p=P)),
            ):
                sp.dma_start(dst, src).then_inc(loaded, 16)
            for dst, src in (
                (w_out[:, :, :], out_wT.rearrange("(j p) n -> p j n", p=P)),
                (w_glu[:, :, :], glu_wT.rearrange("(f p) n -> p f n", p=P)),
                (w_r[:, :, :], router_w.rearrange("(f p) n -> p f n", p=P)),
                (w_sgu[:, :, :], sgu_w.rearrange("(f p) n -> p f n", p=P)),
                (w_sd[:, :, :], sdown_w.rearrange("(k p) n -> p k n", p=P)),
            ):
                sp.dma_start(dst, src).then_inc(post_loaded, 16)

            def at(v, q):
                return v[q] if isinstance(q, int) else v[bass.ds(q, 1)].squeeze(0)

            def turn(b, h, prep, post, finish):
                if finish:
                    store_out(b - 2)
                if prep:
                    keep_x(b + 1, 1 - h)
                if not isinstance(b, int) or b + 2 < B:
                    load_x(b + 2)
                if post:
                    store(b - 1, 1 - h)

            def store(q, h):
                sp.wait_ge(post_read, q * POST_USES + POST_C + 1)
                sp.dma_start(at(counts_v, q), cnt[h][:, :]).then_inc(counts_stored, 16)
                if isinstance(q, int) and q == B - 1:
                    sp.wait_ge(counts_ready, B)
                    sp.dma_start(ends.rearrange("(e t) -> e t", t=TILES), tile_ends[:, :]).then_inc(ends_stored, 16)
                sp.wait_ge(route, ROUTES * q + ROUTES)
                sp.dma_start(at(table_v, q), rows[:, :, :]).then_inc(rows_stored, 16)

            def store_out(q):
                sp.wait_ge(post_read, q * POST_USES + POST_USES)
                sp.dma_start(at(out_v, q), outb.rearrange("p (i d) -> p i d", i=NT)).then_inc(out_stored, 16)

            def keep_x(p, h):
                sp.wait_ge(x_summed, p + 1)
                if not (isinstance(p, int) and p < 2):
                    sp.wait_ge(post_read, (p - 2) * POST_USES + POST_MT + 1)
                sp.dma_start(xs[h][:, :, :], xin[:, :, :]).then_inc(xs_ready, 16)

            keep_x(0, 0)
            load_x(1)
            turns(sp, turn)
            store_out(B - 2)
            store(B - 1, 1)
            sp.wait_ge(consts, CONSTS)
            sp.dma_start(out[T:T + CAP, :], xd[:, 0:DM]).then_inc(pad_stored, 16)
            sp.wait_ge(ends_stored, 16)
            sp.wait_ge(summed, B * N)
            for c in range(CHUNKS):
                sp.dma_start(big[:, c * CHUNK * TILES:(c + 1) * CHUNK * TILES],
                             ends.rearrange("(a n) -> a n", a=1)[:, c * CHUNK * TILES:(c + 1) * CHUNK * TILES]
                             .broadcast_to([P, CHUNK * TILES])).then_inc(ends_back[c], 16)
            sp.wait_ge(state_ready, B * N)

            def weights(e, r):
                wait(sp, e_o, e - ER + 1)
                a, d = (egu_w[e], edown_w[e]) if isinstance(e, int) else (
                    egu_w[bass.ds(e, 1)].squeeze(0), edown_w[bass.ds(e, 1)].squeeze(0))
                sp.dma_start(ewg[r], a.rearrange("(f p) n -> p f n", p=P)).then_inc(e_weights[r], 16)
                sp.dma_start(ewd[r], d).then_inc(e_weights[r], 16)

            for e in range(ER):
                weights(e, e)
            store_out(B - 1)
            with sp.Fori(1, E // ER) as it:
                for r in range(ER):
                    weights(it * ER + r, r)
            sp.wait_ge(rows_stored, 16 * B)
            sp.wait_ge(out_stored, 16 * B)
            sp.wait_ge(counts_stored, 16 * B)
            sp.wait_ge(pad_stored, 16)
            sp.wait_ge(e_scattered, 16 * E)

        @block.gpsimd
        def _(pool):
            pool.memset(ident[:, :], 0.0).then_inc(cleared, 1)
            pool.memset(onehot[:, :], 0.0).then_inc(cleared, 1)
            pool.memset(steps_tri[:, :], 1.0).then_inc(cleared, 1)
            pool.memset(w_x[:, :, R:32], 0.0).then_inc(cleared, 1)
            pool.memset(w_dt[:, :], 0.0).then_inc(cleared, 1)
            pool.memset(minus_half[:, :], -0.5).then_inc(cleared, 1)
            pool.wait_ge(cleared, 6)
            pool.affine_select(out=ident[:, :], in_=ident[:, :], compare_op=ALU.not_equal, fill=1.0,
                               base=0, pattern=[[-1, P]], channel_multiplier=1).then_inc(consts, 1)
            for c in range(1, 4):
                if c > 1:
                    pool.wait_ge(consts, c)
                pool.affine_select(out=onehot[:, :], in_=onehot[:, :], compare_op=ALU.not_equal, fill=1.0,
                                   base=-32 * c, pattern=[[-1, 2 * N]], channel_multiplier=1).then_inc(consts, 1)
            pool.affine_select(out=steps_tri[:, :], in_=steps_tri[:, :], compare_op=ALU.is_ge, fill=0.0,
                               base=-3 * P, pattern=[[1, 3 * P + L]], channel_multiplier=-1).then_inc(consts, 1)
            pool.iota(slot[:, :], pattern=[[0, 1]], base=0, channel_multiplier=1,
                      allow_small_or_imprecise_dtypes=True).then_inc(consts, 1)
            pool.iota(slot_pad[:, :], pattern=[[0, 1]], base=T, channel_multiplier=1,
                      allow_small_or_imprecise_dtypes=True).then_inc(consts, 1)
            pool.iota(row_of[:, :], pattern=[[TILES, E]], base=0, channel_multiplier=0,
                      allow_small_or_imprecise_dtypes=True).then_inc(consts, 1)

            def scan_input(b, h, n):
                g = b * N + n
                if n == 0:
                    pool.wait_ge(dt_ready, 2 * b + 2)
                pool.wait_ge(b_copied, g + 1)
                wait(pool, summed, g - HR + 1)
                pool.tensor_tensor(hs[:, n % HR], dtu[h][:, :, :],
                                   b_all[:, n % 2, :].unsqueeze(1).broadcast_to([P, J, L]), ALU.mult)\
                    .then_inc(input_ready, 1)

            def scales(s, which, k):
                wait_apart(pool, s, 3 * k + 2)
                pool.tensor_scalar(rstd[:, which, :].unsqueeze(2), mv[:, which, :, 1:2], EPS, None, ALU.add)\
                    .then_inc(rstd_ready[which], 1)
                pool.wait_ge(rstd_ready[which], 2 * k + 1)
                pool.tensor_tensor(rstd[:, which, :], rstd[:, which, :], minus_half[:, :], ALU.pow)\
                    .then_inc(rstd_ready[which], 1)

            def add_norm(p):
                pool.wait_ge(ln0, 3 * p + 3)
                pool.tensor_tensor(xin[:, :, :], xin[:, :, :], xn[:, :, :], ALU.add).then_inc(x_summed, 1)

            def split_bc(p, h):
                wait_apart(pool, prep_read, PREP_USES * p + PREP_S + 1)
                pool.tensor_copy(parts[h][:, :], xd[:, :]).then_inc(split, 1)
                pool.wait_ge(split, 4 * p + 1)
                pool.tensor_tensor(xd[64:128, :], xd[64:128, :], parts[h][64:128, :], ALU.subtract).then_inc(split, 1)
                wait_apart(pool, split, 4 * p + 2)
                pool.tensor_copy(parts[h][64:128, :], xd[64:128, :]).then_inc(split, 1)
                pool.wait_ge(split, 4 * p + 3)
                pool.tensor_tensor(parts[h][96:128, :], xd[96:128, :], parts[h][96:128, :], ALU.subtract)\
                    .then_inc(split, 1)
                pool.wait_ge(split, 4 * p + 4)

            def step_sizes(p, h):
                pool.wait_ge(soft, 2 * p + 2)
                pool.tensor_tensor(dt[h][:, :, :], dt[h][:, :, :], ab, ALU.add).then_inc(dt_ready, 1)

            def step_inputs(p, h):
                pool.wait_ge(dt_ready, 2 * p + 1)
                pool.tensor_tensor(dtu[h][:, :, :], dt[h][:, :, :], xc[:, :, :], ALU.mult).then_inc(dt_ready, 1)

            def turn(b, h, prep, post, finish):
                for n in range(N):
                    if prep and n == 0:
                        scales(ln0, 0, b + 1)
                    if prep and n == 2:
                        add_norm(b + 1)
                        scales(ln1, 1, b + 1)
                    if post and n == LN2_SLOT:
                        scales(ln2, 2, b - 1)
                    if n < N - 2:
                        scan_input(b, h, n + 2)
                    elif prep:
                        scan_input(b + 1, 1 - h, n + 2 - N)
                    if prep and n == SPLIT_SLOT:
                        split_bc(b + 1, 1 - h)
                    if prep and n == STEP_SLOT:
                        step_sizes(b + 1, 1 - h)
                    if prep and n == DTU_SLOT:
                        step_inputs(b + 1, 1 - h)

            scales(ln0, 0, 0)
            add_norm(0)
            scales(ln1, 1, 0)
            split_bc(0, 0)
            step_sizes(0, 0)
            step_inputs(0, 0)
            scan_input(0, 0, 0)
            scan_input(0, 0, 1)
            turns(pool, turn)
            scales(ln2, 2, B - 1)

            pool.wait_ge(split, 4 * B)
            pool.wait_ge(prep_full, B * PREP_USES)
            pool.memset(xd[:, 0:DM], 0.0).then_inc(consts, 1)
            def gather_tile(e, r):
                wait_apart(pool, tile_ready, e + 1)
                pool.indirect_dma_start(out=tile_counts[r], out_offset=None, in_=tiles,
                                        in_offset=bass.IndirectOffsetOnAxis(ap=ring_tile[r], axis=0))\
                    .then_inc(t_gathered[r], 16)

            tiles = counts.rearrange("e (t k) -> (e t) k", k=P)
            pool.wait_ge(counts_stored, 16 * B)
            for e in range(TILE_AHEAD):
                gather_tile(e, e)
            pool.wait_ge(rows_stored, 16 * B)

            def gather(e, r):
                pool.wait_ge(ring_ready, e + 1)
                if not (isinstance(e, int) and e < ER):
                    wait_apart(pool, e_res, e - ER + 1)
                pool.indirect_dma_start(out=got[r % ER], out_offset=None, in_=table,
                                        in_offset=bass.IndirectOffsetOnAxis(ap=ring_in[r], axis=0))\
                    .then_inc(e_gathered[r % ER], 16)

            def scatter(e, r):
                pool.wait_ge(e_res, e + 1)
                if not (isinstance(e, int) and e == 0):
                    wait_apart(pool, e_scattered, e * 16)
                pool.indirect_dma_start(out=out, out_offset=bass.IndirectOffsetOnAxis(ap=ring_out[r], axis=0),
                                        in_=res_e[r % ER], in_offset=None, compute_op=ALU.add).then_inc(e_scattered, 16)

            def expert(e, k):
                if not (isinstance(e, int) and e + AHEAD >= E):
                    gather(e + AHEAD, (k + AHEAD) % IR)
                scatter(e, k)
                if not (isinstance(e, int) and e + TILE_AHEAD >= E):
                    gather_tile(e + TILE_AHEAD, (k + TILE_AHEAD) % IR)

            for e in range(AHEAD):
                gather(e, e)
            pool.wait_ge(out_stored, 16 * B)
            pool.wait_ge(pad_stored, 16)
            for e in range(IR):
                expert(e, e)
            with pool.Fori(1, E // IR - 1) as it:
                for k in range(IR):
                    expert(it * IR + k, k)
            for e in range(E - IR, E):
                expert(e, e % IR)
            pool.wait_ge(e_scattered, 16 * E)

        @block.scalar
        def _(act):
            act.wait_ge(loaded, 16 * LOADS)
            act.activation(neg_a[:, :, :], neg_a[:, :, :], ACT.Exp).then_inc(made, 1)

            def copy_b(g, n):
                act.wait_ge(b_full, g + 1)
                wait(act, input_ready, g - 1)
                act.copy(b_all[:, n % 2, :], bcbank).then_inc(b_copied, 1)

            def copy_c(g, n):
                act.wait_ge(c_full, g + 1)
                wait(act, readout_ready, g - 1)
                act.copy(c_all[:, n % 2, :], bcbank).then_inc(c_copied, 1)

            def decays(b, h, n, blocks):
                g = b * N + n
                if 0 in blocks:
                    if n == 0:
                        act.wait_ge(dt_ready, 2 * b + 1)
                    wait(act, state_ready, g - 1)
                for j in blocks:
                    i = act.activation(decay[:, n % 2, j, 1:L], dt[h][:, j, 1:L], ACT.Exp, scale=neg_a[:, j, n:n + 1])
                if J - 1 in blocks:
                    i.then_inc(decay_ready, 1)

            def read_xnT(p, f):
                act.wait_ge(prep_full, p * PREP_USES + PREP_T + f + 1)
                act.activation(xnT[:, f, :], prbank, ACT.Identity, bias=b_sb[:, f:f + 1],
                               scale=g_sb[:, f:f + 1]).then_inc(prep_read, 1)

            def read_xp(p, j):
                act.wait_ge(prep_full, p * PREP_USES + PREP_X + j + 1)
                wait(act, dt_ready, 2 * p)
                act.copy(xpad[:, j, PAD:PAD + L], prbank)
                if j == 0:
                    wait(act, summed, (p - 1) * N + 1)
                act.activation(xc[:, j, :], prbank, ACT.Identity, bias=cb_sb[:, j:j + 1],
                               scale=cw_sb[:, j, PAD:TAPS]).then_inc(prep_read, 1)

            def read_z(p, h, j):
                act.wait_ge(prep_full, p * PREP_USES + PREP_Z + j + 1)
                wait(act, post_full, (p - 2) * POST_USES + POST_M + 1)
                act.copy(sz[h][:, j, :], prbank).then_inc(prep_read, 1)

            def silus(p, h):
                act.wait_ge(prep_read, p * PREP_USES + PREP_Z + J)
                act.wait_ge(conv_step, (p + 1) * J * PAD)
                act.activation(xc[:, :, :], xc[:, :, :], ACT.Silu).then_inc(xc_ready, 1)
                act.activation(sz[h][:, :, :], sz[h][:, :, :], ACT.Silu).then_inc(z_ready, 1)

            def read_xd(p):
                act.wait_ge(prep_full, p * PREP_USES + PREP_S + 1)
                wait(act, split, 4 * p)
                act.copy(xd[:, :], prbank).then_inc(prep_read, 1)

            def read_dt(p, h, j):
                act.wait_ge(prep_full, p * PREP_USES + PREP_D + j + 1)
                wait(act, state_ready, (p - 1) * N)
                act.activation(ab[:, j, :], prbank, ACT.Abs, bias=db_sb[:, j:j + 1])
                act.activation(dt[h][:, j, :], prbank, ACT.Relu, bias=db_sb[:, j:j + 1]).then_inc(prep_read, 1)

            def soft_exp(p):
                act.wait_ge(prep_read, p * PREP_USES + PREP_USES)
                act.activation(ab, ab, ACT.Exp, scale=-1.0).then_inc(soft, 1)

            def soft_log(p):
                act.wait_ge(soft, 2 * p + 1)
                act.activation(ab, ab, ACT.Ln, bias=1.0).then_inc(soft, 1)

            def gelu(q):
                act.wait_ge(post_full, q * POST_USES + POST_M + 1)
                wait(act, out_stored, 16 * q)
                act.activation(mT[:, :, :], pobank, ACT.Gelu).then_inc(post_read, 1)

            def glu_gate(q):
                wait(act, post_read, q * POST_USES)
                act.wait_ge(post_full, q * POST_USES + POST_G + 1)
                for f in range(FM):
                    i = act.activation(sg[:, f, :], pobank[:, f, :], ACT.Sigmoid, bias=gb_sb[:, FM + f:FM + f + 1])
                i.then_inc(post_read, 1)

            def read_x2T(q):
                act.wait_ge(post_full, q * POST_USES + POST_XT + 1)
                act.copy(x2T[:, :, :], pobank).then_inc(post_read, 1)

            def router_exp(q):
                act.wait_ge(route, q * ROUTES + 2)
                for i in range(NT):
                    act.activation(pr[:, i, :], lg[:, i, 0:E], ACT.Exp, bias=negmax[:, i:i + 1],
                                   accum_out=esum[:, i:i + 1])
                act.activation(eg.unsqueeze(2), lg[:, :, E:E + 1], ACT.Exp, scale=-1.0).then_inc(exp_ready, 1)

            def read_counts(q, h):
                act.wait_ge(post_full, q * POST_USES + POST_C + 1)
                wait(act, counts_stored, 16 * q)
                act.wait_ge(made, MADE)
                act.activation(cnt[h][:, :], pobank[0:E, 0, :], ACT.Identity, bias=cnt[1 - h][:, L - 1:L])\
                    .then_inc(post_read, 1)
                act.wait_ge(post_read, q * POST_USES + POST_C + 1)
                act.copy(tile_ends[:, bass.ds(q * NT, NT)], cnt[h][:, P - 1:L:P]).then_inc(counts_ready, 1)

            def read_gates(q, k):
                act.wait_ge(post_full, q * POST_USES + (POST_SG, POST_SG2)[k] + 1)
                act.copy(hid[:, 2 * k:2 * k + 2, :], pobank).then_inc(post_read, 1)

            def hid_silu(q):
                act.wait_ge(post_read, q * POST_USES + POST_SG2 + 1)
                act.activation(hid[:, :, :], hid[:, :, :], ACT.Silu).then_inc(hid_ready, 1)

            def prep_at(p, h, at):
                for f in range(FM):
                    if at == T_AT[f]:
                        read_xnT(p, f)
                for j in range(J):
                    if at == X_AT[j]:
                        read_xp(p, j)
                    if at == Z_AT[j]:
                        read_z(p, h, j)
                    if at == D_AT[j]:
                        read_dt(p, h, j)
                if at == SILU_AT:
                    silus(p, h)
                if at == PX_AT[1]:
                    read_xd(p)
                if at == SOFT_AT[0]:
                    soft_exp(p)
                if at == SOFT_AT[1]:
                    soft_log(p)

            def post_at(q, h, at):
                if at == M_AT[3]:
                    gelu(q)
                if at == G_AT[1]:
                    glu_gate(q)
                if at == XT_AT:
                    read_x2T(q)
                if at == EXP_AT:
                    router_exp(q)
                if at == SG_AT[1]:
                    read_gates(q, 0)
                if at == C_AT:
                    read_counts(q, h)
                if at == SG_AT[3]:
                    read_gates(q, 1)
                if at == HID_AT:
                    hid_silu(q)

            def turn(b, h, prep, post, finish):
                p, q = b + 1, b - 1

                def others(at):
                    if prep:
                        prep_at(p, 1 - h, at)
                    if post:
                        post_at(q, 1 - h, at)

                for n in range(N):
                    g = b * N + n
                    ahead = (b, h, n + 2) if n < N - 2 else (p, 1 - h, n + 2 - N)
                    more = n < N - 2 or prep
                    if more:
                        decays(*ahead, (0, 1))
                    others((n, 1))
                    if n < N - 3 or prep:
                        copy_b(g + 3, n + 1)
                    if more:
                        decays(*ahead, (2,))
                    others((n, 2))
                    if more:
                        copy_c(g + 2, n)
                        decays(*ahead, (3,))
                    others((n, 3))

            act.wait_ge(made, MADE)
            places = [(n, k) for n in range(N) for k in (1, 2, 3)]
            for at in places:
                prep_at(0, 0, at)
            for n in range(2):
                copy_b(n, n)
                copy_c(n, n)
                decays(0, 0, n, range(J))
            copy_b(2, 2)
            turns(act, turn)
            for at in places:
                post_at(B - 1, 1, at)

            def copy_rows(e, r):
                act.wait_ge(e_t, e + 1)
                wait(act, e_gu, e - 1)
                act.copy(geT[r % 2], ps[:, r % 2, 0:DM].rearrange("p (f n) -> p f n", f=FM)).then_inc(e_tc, 1)

            def gate(e, r):
                act.wait_ge(e_gu, e + 1)
                wait(act, e_hid, e - 1)
                act.activation(act_e[r % 2], ps[:, 2 + r % 2, 0:IE], ACT.Silu).then_inc(e_act, 1)

            copy_rows(0, 0)
            for e in range(ER):
                gate(e, e)
                copy_rows(e + 1, e + 1)
            with act.Fori(1, E // ER - 1) as it:
                for r in range(ER):
                    gate(it * ER + r, r)
                    copy_rows(it * ER + r + 1, r + 1)
            for e in range(E - ER, E):
                gate(e, e)
                if e + 1 < E:
                    copy_rows(e + 1, e + 1)

        @block.tensor
        def _(pe):
            def one_row(h, row):
                return pe.matmul(bcbank, onehot[:, row:row + 1].broadcast_to([P, P]), parts[h][:, :],
                                 start=True, stop=True)

            def broadcast_b(g, h, n):
                wait(pe, c_copied, g - 1 if not isinstance(g, int) or g > 2 else g)
                if isinstance(g, int) and g == 3:
                    pe.wait_ge(b_copied, 3)
                one_row(h, n).then_inc(b_full, 1)

            def broadcast_c(g, h, n):
                last = isinstance(g, int) and g == B * N - 1
                pe.wait_ge(b_copied, g + 1 if last else g + 2)
                if last:
                    pe.wait_ge(c_copied, g)
                one_row(h, N + n).then_inc(c_full, 1)

            def start_y(b):
                pe.wait_ge(xc_ready, b + 1)
                wait(pe, y_read, b)
                for j in range(J):
                    pe.matmul(ybank[:, j, :], d_diag[:, j, :], xc[:, j, :], start=True, stop=False)

            def sum_states(g, n, j):
                if j == 0:
                    pe.wait_ge(readout_ready, g + 1)
                i = pe.matmul(ybank[:, j, :], ident[:, :], hs[:, n % HR, j, :], start=False, stop=(n == N - 1))
                if j == J - 1:
                    i.then_inc(summed, 1)

            def use_prep(p, u):
                wait(pe, prep_read, p * PREP_USES + u)

            def turn_xn(p, f):
                pe.wait_ge(ln1, 3 * p + 3)
                use_prep(p, PREP_T + f)
                for i in range(NT):
                    m = pe.transpose(prbank[:, i * P:(i + 1) * P], xn[:, i, f * P:(f + 1) * P], ident[:, :])
                m.then_inc(prep_full, 1)

            def project_in(p, u, col):
                pe.wait_ge(prep_read, p * PREP_USES + PREP_T + FM)
                use_prep(p, u)
                for f in range(FM):
                    m = pe.matmul(prbank, w_in[:, f, col * P:(col + 1) * P], xnT[:, f, :],
                                  start=(f == 0), stop=(f == FM - 1))
                m.then_inc(prep_full, 1)

            def project_x(p, half):
                if half == 0:
                    pe.wait_ge(xc_ready, p + 1)
                    use_prep(p, PREP_S)
                for j in (2 * half, 2 * half + 1):
                    m = pe.matmul(prbank, w_x[:, j, :], xc[:, j, :], start=(j == 0), stop=(j == J - 1))
                if half == 1:
                    m.then_inc(prep_full, 1)

            def project_dt(p, j):
                if j == 0:
                    pe.wait_ge(prep_read, p * PREP_USES + PREP_S + 1)
                use_prep(p, PREP_D + j)
                pe.matmul(prbank, w_dt[:, j * P:(j + 1) * P], xd[0:2 * R, :], start=True, stop=True)\
                    .then_inc(prep_full, 1)

            def use_post(q, u):
                wait(pe, post_read, q * POST_USES + u)

            def project_out(q, h, c):
                f, half = c // 2, c % 2
                if c == 0:
                    pe.wait_ge(y_read, q + 1)
                    use_post(q, POST_M)
                for j in (2 * half, 2 * half + 1):
                    m = pe.matmul(pobank[:, f, :], w_out[:, j, f * P:(f + 1) * P], sz[h][:, j, :],
                                  start=(j == 0), stop=(j == J - 1))
                if c == 3:
                    m.then_inc(post_full, 1)

            def project_glu(q, u, half, f):
                if f == 0:
                    use_post(q, u)
                for k in range(FM):
                    col = (half * FM + f) * P
                    m = pe.matmul(pobank[:, f, :], w_glu[:, k, col:col + P], mT[:, k, :],
                                  start=(k == 0), stop=(k == FM - 1))
                if f == FM - 1:
                    m.then_inc(post_full, 1)

            def turn_m(q):
                use_post(q, POST_MT)
                for i in range(NT):
                    for f in range(FM):
                        m = pe.transpose(po_tok[:, i, f * P:(f + 1) * P], sg[:, f, i * P:(i + 1) * P], ident[:, :])
                m.then_inc(post_full, 1)

            def turn_x2(q):
                pe.wait_ge(ln2, 3 * q + 3)
                use_post(q, POST_XT)
                for f in range(FM):
                    for i in range(NT):
                        m = pe.transpose(pobank[:, f, i * P:(i + 1) * P], rows[:, i, f * P:(f + 1) * P], ident[:, :])
                m.then_inc(post_full, 1)

            def logits(q):
                use_post(q, POST_R)
                for i in range(NT):
                    for f in range(FM):
                        m = pe.matmul(pobank[:, 0, i * P:i * P + E + 1], x2T[:, f, i * P:(i + 1) * P], w_r[:, f, :],
                                      start=(f == 0), stop=(f == FM - 1))
                m.then_inc(post_full, 1)

            def count(q):
                pe.wait_ge(route, q * ROUTES + MASK_STEP)
                use_post(q, POST_C)
                for i in range(NT):
                    at = (NT - 1 - i) * P
                    m = pe.matmul(pobank[0:E, 0, :], maskb[:, i, :], steps_tri[:, at:at + L],
                                  start=(i == 0), stop=(i == NT - 1))
                m.then_inc(post_full, 1)

            def shared_up(q, u, block, k):
                if k == 0:
                    use_post(q, u)
                for f in range(FM):
                    m = pe.matmul(pobank[:, k, :], w_sgu[:, f, block * P:(block + 1) * P], x2T[:, f, :],
                                  start=(f == 0), stop=(f == FM - 1))
                if k == 1:
                    m.then_inc(post_full, 1)

            def shared_down(q, i):
                if i == 0:
                    use_post(q, POST_DN)
                for k in range(KS):
                    m = pe.matmul(po_tok[:, i, :], hid[:, k, i * P:(i + 1) * P], w_sd[:, k, :],
                                  start=(k == 0), stop=(k == KS - 1))
                if i == NT - 1:
                    m.then_inc(post_full, 1)

            def prep_at(p, at):
                for f in range(FM):
                    if at == T_AT[f]:
                        turn_xn(p, f)
                for j in range(J):
                    if at == X_AT[j]:
                        project_in(p, PREP_X + j, j)
                    if at == Z_AT[j]:
                        project_in(p, PREP_Z + j, J + j)
                    if at == D_AT[j]:
                        project_dt(p, j)
                for half in range(2):
                    if at == PX_AT[half]:
                        project_x(p, half)

            def post_at(q, h, at):
                for c in range(4):
                    if at == M_AT[c]:
                        project_out(q, h, c)
                for f in range(FM):
                    if at == G_AT[f]:
                        project_glu(q, POST_G, 1, f)
                    if at == V_AT[f]:
                        project_glu(q, POST_V, 0, f)
                if at == MT_AT:
                    turn_m(q)
                if at == XT_AT:
                    turn_x2(q)
                if at == R_AT:
                    logits(q)
                if at == C_AT:
                    count(q)
                for k in range(KS):
                    if at == SG_AT[k]:
                        shared_up(q, (POST_SG, POST_SG2)[k // 2], k, k % 2)
                    if at == SU_AT[k]:
                        shared_up(q, (POST_SU, POST_SU2)[k // 2], KS + k, k % 2)
                if at == DN_AT[0]:
                    shared_down(q, 0)

            def finish_at(q, at):
                for i in range(1, NT):
                    if at == DN_AT[i]:
                        shared_down(q, i)

            def turn(b, h, prep, post, finish):
                p, q = b + 1, b - 1

                def others(at):
                    if finish:
                        finish_at(q - 1, at)
                    if prep:
                        prep_at(p, at)
                    if post:
                        post_at(q, 1 - h, at)

                for n in range(N):
                    g = b * N + n
                    others((n, 1))
                    if n == 0:
                        start_y(b)
                    sum_states(g, n, 0)
                    if n < N - 3:
                        broadcast_b(g + 3, h, n + 3)
                    elif prep:
                        if n == N - 3:
                            pe.wait_ge(split, 4 * p + 4)
                        broadcast_b(g + 3, 1 - h, n + 3 - N)
                    sum_states(g, n, 1)
                    others((n, 2))
                    sum_states(g, n, 2)
                    if n < N - 2:
                        broadcast_c(g + 2, h, n + 2)
                    elif prep:
                        broadcast_c(g + 2, 1 - h, n + 2 - N)
                    sum_states(g, n, 3)
                    others((n, 3))

            pe.wait_ge(loaded, 16 * LOADS)
            pe.wait_ge(consts, 8)
            pe.wait_ge(made, MADE)
            places = [(n, k) for n in range(N) for k in (1, 2, 3)]
            for at in places:
                prep_at(0, at)
            pe.wait_ge(split, 4)
            for n in range(2):
                broadcast_b(n, 0, n)
                pe.wait_ge(b_copied, n + 1)
                one_row(0, N + n).then_inc(c_full, 1)
            pe.wait_ge(c_copied, 2)
            broadcast_b(2, 0, 2)
            pe.wait_ge(post_loaded, 16 * POST_LOADS)
            turns(pe, turn)
            for at in places:
                finish_at(B - 2, at)
                post_at(B - 1, 1, at)
            for at in places:
                finish_at(B - 1, at)

            def turn_rows(e, r, turn):
                pe.wait_ge(e_gathered[r], turn * 16 + 16)
                wait(pe, e_tc, e - 1)
                for f in range(FM):
                    m = pe.transpose(ps[:, r % 2, f * P:(f + 1) * P], got[r][:, f * P:(f + 1) * P], ident[:, :])
                m.then_inc(e_t, 1)

            def gate_up(e, r, turn):
                pe.wait_ge(e_weights[r], turn * 32 + 32)
                pe.wait_ge(e_tc, e + 1)
                wait(pe, e_hid, e - 1)
                for half in range(2):
                    for f in range(FM):
                        m = pe.matmul(ps[:, 2 + r % 2, half * IE:(half + 1) * IE],
                                      ewg[r][:, f, half * IE:(half + 1) * IE], geT[r % 2][:, f, :],
                                      start=(f == 0), stop=(f == FM - 1))
                m.then_inc(e_gu, 1)

            def down(e, r):
                pe.wait_ge(e_hid, e + 1)
                wait(pe, e_res, e - 1)
                pe.matmul(ps[:, 4 + r % 2, 0:DM], hid_e[r % 2], ewd[r], start=True, stop=True).then_inc(e_o, 1)

            def experts(first, turn, count):
                for r in range(ER):
                    gate_up(first + r, r, turn)
                    if r + 1 < count:
                        turn_rows(first + r + 1, (r + 1) % ER, turn if r + 1 < ER else turn + 1)
                    down(first + r, r)

            turn_rows(0, 0, 0)
            experts(0, 0, ER + 1)
            with pe.Fori(1, E // ER - 1) as it:
                experts(it * ER, it, ER + 1)
            experts(E - ER, E // ER - 1, ER)

        @block.vector
        def _(dve):
            for k, t in enumerate((decay[:, :, :, 0:1], xpad[:, :, 0:PAD], cnt[1][:, L - 1:L])):
                dve.memset(t, 0.0).then_inc(made, 1)
            dve.wait_ge(loaded, 16 * LOADS)
            dve.wait_ge(made, 4)
            dve.tensor_scalar(neg_a[:, :, :], neg_a[:, :, :], -1.0, None, ALU.mult).then_inc(made, 1)
            dve.wait_ge(consts, 8)
            for j in range(J):
                dve.tensor_scalar(d_diag[:, j, :], ident[:, :], d_sb[:, j:j + 1], None, ALU.mult).then_inc(made, 1)

            def moments(s, which, k, src):
                for i in range(NT):
                    m = dve.bn_stats(stats[:, which, i, :], src[:, i, :])
                m.then_inc(s, 1)
                wait_apart(dve, s, 3 * k + 1)
                for i in range(NT):
                    m = dve.bn_aggr(mv[:, which, i, :], stats[:, which, i, :])
                m.then_inc(s, 1)

            def normalise(s, which, k, src, dst):
                dve.wait_ge(rstd_ready[which], 2 * k + 2)
                for i in range(NT):
                    m = dve.tensor_scalar(dst[:, i, 0:DM], src[:, i, :], mv[:, which, i, 0:1],
                                          rstd[:, which, i:i + 1], ALU.subtract, ALU.mult)
                m.then_inc(s, 1)

            def moments_x(p):
                dve.wait_ge(x_loaded, 16 * p + 16)
                moments(ln0, 0, p, xin)

            def norm_x(p):
                wait(dve, prep_full, (p - 1) * PREP_USES + PREP_T + FM)
                wait(dve, post_read, (p - 2) * POST_USES)
                normalise(ln0, 0, p, xin, xn)
                dve.wait_ge(ln0, 3 * p + 3)
                moments(ln1, 1, p, xn)

            def norm_again(p):
                dve.wait_ge(x_summed, p + 1)
                normalise(ln1, 1, p, xn, xn)

            def conv(p, j):
                dve.wait_ge(prep_read, p * PREP_USES + PREP_X + j + 1)
                for k in range(PAD):
                    if k > 0:
                        dve.wait_ge(conv_step, (p * J + j) * PAD + k)
                    dve.scalar_tensor_tensor(xc[:, j, :], xpad[:, j, k:k + L], cw_sb[:, j, k:k + 1], xc[:, j, :],
                                             ALU.mult, ALU.add).then_inc(conv_step, 1)

            def gate_y(q, h):
                dve.wait_ge(summed, (q + 1) * N)
                dve.wait_ge(z_ready, q + 1)
                dve.tensor_tensor(sz[h][:, :, :], ybank, sz[h][:, :, :], ALU.mult).then_inc(y_read, 1)

            def glu(q):
                dve.wait_ge(post_full, q * POST_USES + POST_V + 1)
                dve.wait_ge(post_read, q * POST_USES + POST_G + 1)
                for f in range(FM):
                    i = dve.scalar_tensor_tensor(sg[:, f, :], pobank[:, f, :], gb_sb[:, f:f + 1], sg[:, f, :],
                                                 ALU.add, ALU.mult)
                i.then_inc(post_read, 1)

            def add_m(q, h):
                dve.wait_ge(post_full, q * POST_USES + POST_MT + 1)
                dve.wait_ge(xs_ready, 16 * q + 16)
                dve.tensor_tensor(x1[:, :, :], po_tok, xs[h][:, :, :], ALU.add).then_inc(post_read, 1)

            def moments_x1(q):
                dve.wait_ge(post_read, q * POST_USES + POST_MT + 1)
                moments(ln2, 2, q, x1)

            def norm_x1(q):
                wait(dve, rows_stored, 16 * q)
                normalise(ln2, 2, q, x1, rows)

            def read_logits(q):
                dve.wait_ge(post_full, q * POST_USES + POST_R + 1)
                dve.tensor_copy(lg[:, :, :], pobank[:, 0, :].rearrange("p (i c) -> p i c", i=NT)[:, :, 0:E + 1])\
                    .then_inc(post_read, 1)
                dve.wait_ge(post_read, q * POST_USES + POST_R + 1)
                dve.tensor_reduce(negmax, lg[:, :, 0:E], AX.X, ALU.max, negate=True).then_inc(route, 2)

            def choose(q):
                at = [q * ROUTES + 2]

                def link(i):
                    i.then_inc(route, 1)
                    at[0] = at[0] + 1
                    wait_apart(dve, route, at[0])

                def wide(t, w):
                    return t.unsqueeze(2).broadcast_to([P, NT, w])

                dve.wait_ge(exp_ready, q + 1)
                dve.reciprocal(rsum, esum)
                link(dve.tensor_scalar(gate_s, eg, 1.0, None, ALU.add))
                dve.reciprocal(gate_s, gate_s)
                link(dve.tensor_tensor(pr[:, :, :], pr[:, :, :], wide(rsum, E), ALU.mult))
                for i in range(NT):
                    k = dve.max(top[:, i, :], pr[:, i, :])
                link(k)
                for i in range(NT):
                    dve.match_replace(rep[:, i, :], top[:, i, :], pr[:, i, :], -1.0)
                link(dve.tensor_reduce(s8, top[:, :, :], AX.X, ALU.add))
                dve.reciprocal(s8, s8)
                link(dve.tensor_tensor(rep[:, :, :], rep[:, :, :], pr[:, :, :], ALU.not_equal))
                link(dve.tensor_copy(maskb[:, :, :], rep[:, :, :]))
                link(dve.tensor_tensor(pr[:, :, :], pr[:, :, :], rep[:, :, :], ALU.mult))
                dve.tensor_tensor(rows[:, :, DM:ROW], pr[:, :, :], wide(s8, E), ALU.mult).then_inc(route, 1)

            def mul_up(q, k):
                dve.wait_ge(post_full, q * POST_USES + POST_SU + k + 1)
                if k == 0:
                    dve.wait_ge(hid_ready, q + 1)
                dve.tensor_tensor(hid[:, 2 * k:2 * k + 2, :], pobank, hid[:, 2 * k:2 * k + 2, :], ALU.mult)\
                    .then_inc(post_read, 1)

            def add_shared(q):
                dve.wait_ge(post_full, q * POST_USES + POST_DN + 1)
                for i in range(NT):
                    k = dve.scalar_tensor_tensor(outb[:, i * DM:(i + 1) * DM], po_tok[:, i, :], gate_s[:, i:i + 1],
                                                 x1[:, i, :],
                                                 ALU.mult, ALU.add)
                k.then_inc(post_read, 1)

            def after_step(q, h, n):
                if n == UP_SLOTS[0]:
                    mul_up(q, 0)
                if n == UP_SLOTS[1]:
                    mul_up(q, 1)
                if n == GLU_SLOT:
                    glu(q)
                if n == ADD_SLOT:
                    add_m(q, h)
                    moments_x1(q)
                if n == LN2_SLOT:
                    norm_x1(q)
                if n == LOGIT_SLOT:
                    read_logits(q)
                if n == CHOOSE_SLOT:
                    choose(q)

            def turn(b, h, prep, post, finish):
                p, q = b + 1, b - 1
                for n in range(N):
                    g = b * N + n
                    dve.wait_ge(decay_ready, g + 1)
                    dve.wait_ge(input_ready, g + 1)
                    dve.tensor_tensor_scan(hs[:, n % HR].rearrange("p j l -> p (j l)"),
                                           decay[:, n % 2].rearrange("p j l -> p (j l)"),
                                           hs[:, n % HR].rearrange("p j l -> p (j l)"), 0.0, ALU.mult, ALU.add)\
                        .then_inc(state_ready, 1)
                    if post:
                        if n == 0:
                            gate_y(q, 1 - h)
                    dve.wait_ge(state_ready, g + 1)
                    dve.wait_ge(c_copied, g + 1)
                    dve.tensor_tensor(hs[:, n % HR], hs[:, n % HR],
                                      c_all[:, n % 2, :].unsqueeze(1).broadcast_to([P, J, L]), ALU.mult)\
                        .then_inc(readout_ready, 1)
                    if finish and n == END_SLOT:
                        add_shared(q - 1)
                    if prep:
                        if n == 1:
                            norm_x(p)
                        if n == 2:
                            norm_again(p)
                        for j in range(J):
                            if n == CONV_SLOTS[j]:
                                conv(p, j)
                    if post:
                        after_step(q, 1 - h, n)
                    if n == N - 1 and not (isinstance(b, int) and b + 2 >= B):
                        moments_x(p + 1)

            moments_x(0)
            norm_x(0)
            norm_again(0)
            for j in range(J):
                conv(0, j)
            moments_x(1)
            turns(dve, turn)
            add_shared(B - 2)
            gate_y(B - 1, 1)
            for n in range(N):
                after_step(B - 1, 1, n)

            def find_tiles(c):
                es = slice(c * CHUNK, (c + 1) * CHUNK)
                dve.wait_ge(ends_back[c], 16)
                dve.tensor_scalar(ends3[:, es, :], ends3[:, es, :], slot[:, 0:1], None, ALU.is_le)\
                    .then_inc(slot_step, 1)
                dve.wait_ge(slot_step, 5 * c + 1)
                dve.tensor_reduce(tau[:, es], ends3[:, es, :], AX.X, ALU.add).then_inc(slot_step, 1)
                dve.wait_ge(slot_step, 5 * c + 2)
                dve.tensor_scalar(first[:, es], tau[:, es], float(P), None, ALU.mult).then_inc(slot_step, 1)
                dve.scalar_tensor_tensor(loc[:, es], tau[:, es], float(TILES - 1), row_of[:, es], ALU.min, ALU.add)\
                    .then_inc(slot_step, 1)
                dve.wait_ge(slot_step, 5 * c + 4)
                dve.tensor_copy(idx_tile[:, es], loc[:, es]).then_inc(slot_step, 1)
                dve.wait_ge(slot_step, 5 * c + 5)

            def tile_index(e, k):
                dve.tensor_copy(ring_tile[k], idx_tile[:, bass.ds(e, 1)]).then_inc(tile_ready, 1)

            def find_token(e, k, turn):
                dve.wait_ge(t_gathered[k], turn * 16 + 16)
                dve.tensor_scalar(tile_counts[k], tile_counts[k], slot[:, 0:1], None, ALU.is_le).then_inc(find_step, 1)
                dve.wait_ge(find_step, 3 * e + 1)
                dve.tensor_reduce(token[k % 2], tile_counts[k], AX.X, ALU.add).then_inc(find_step, 1)
                dve.wait_ge(find_step, 3 * e + 2)
                dve.tensor_tensor(token[k % 2], token[k % 2], first[:, bass.ds(e, 1)], ALU.add)\
                    .then_inc(find_step, 1)
                dve.wait_ge(find_step, 3 * e + 3)
                dve.tensor_scalar(ring_in[k], token[k % 2], float(T - 1), None, ALU.min)
                wait(dve, e_scattered, (e - IR + 1) * 16)
                dve.tensor_scalar(ring_out[k], token[k % 2], slot_pad[:, 0:1], None, ALU.min)\
                    .then_inc(ring_ready, 1)

            def expert(e, k):
                r = k % ER
                dve.wait_ge(e_act, e + 1)
                wait(dve, e_o, e - 1)
                dve.tensor_tensor(hid_e[r % 2], ps[:, 2 + r % 2, IE:2 * IE], act_e[r % 2], ALU.mult).then_inc(e_hid, 1)
                dve.wait_ge(e_o, e + 1)
                dve.wait_ge(ring_ready, e + 1)
                dve.tensor_scalar(res_e[r], ps[:, 4 + r % 2, 0:DM], got[r][:, bass.ds(e + DM, 1)], None, ALU.mult)\
                    .then_inc(e_res, 1)

            def step(e, k, turn):
                expert(e, k)
                if not (isinstance(e, int) and e + AHEAD + 1 >= E):
                    find_token(e + AHEAD + 1, (k + AHEAD + 1) % IR, turn if k + AHEAD + 1 < IR else turn + 1)
                if not (isinstance(e, int) and e + TILE_AHEAD + 1 >= E):
                    tile_index(e + TILE_AHEAD + 1, (k + TILE_AHEAD + 1) % IR)

            dve.wait_ge(consts, 8)
            find_tiles(0)
            for e in range(TILE_AHEAD + 1):
                tile_index(e, e)
            add_shared(B - 1)
            for e in range(AHEAD + 1):
                find_token(e, e, 0)
            for e in range(IR):
                step(e, e, 0)
                if 1 <= e < CHUNKS:
                    find_tiles(e)
            with dve.Fori(1, E // IR - 1) as it:
                for k in range(IR):
                    step(it * IR + k, k, it)
            for e in range(E - IR, E):
                step(e, e % IR, E // IR - 1)


CHUNK = 16
CHUNKS = E // CHUNK
AHEAD, TILE_AHEAD = 3, 6
ROUTES, MASK_STEP = 10, 8
CONSTS, MADE = 9, 9
LOADS, POST_LOADS = 9, 5
T_AT = (3, 1), (3, 3)
X_AT = (4, 1), (4, 3), (5, 2), (6, 1)
CONV_SLOTS = 5, 6, 6, 8
Z_AT = (6, 2), (7, 1), (8, 1), (8, 2)
SILU_AT = (8, 3)
PX_AT = (9, 2), (9, 3)
D_AT = (10, 1), (10, 2), (11, 1), (11, 2)
SPLIT_SLOT = 11
SOFT_AT = (11, 3), (12, 2)
STEP_SLOT = 12
DTU_SLOT = 13
M_AT = (1, 2), (1, 3), (1, 3), (2, 1)
G_AT = (3, 2), (3, 3)
V_AT = (4, 2), (4, 3)
GLU_SLOT = 6
MT_AT = (7, 1)
ADD_SLOT = 7
LN2_SLOT = 8
XT_AT = (8, 3)
R_AT = (9, 2)
LOGIT_SLOT = 10
EXP_AT = (10, 3)
CHOOSE_SLOT = 11
SG_AT = (10, 3), (11, 1), (11, 3), (12, 1)
C_AT = (12, 2)
HID_AT = (13, 2)
SU_AT = (13, 1), (13, 3), (14, 3), (15, 1)
UP_SLOTS = 14, 15
DN_AT = (15, 3), (0, 1), (0, 1), (0, 1)
END_SLOT = 1


def kernel(**inputs):
    import concourse.bacc as bacc
    import numpy as np
    from concourse.bass_utils import run_bass_kernel_spmd as run

    nc = bacc.Bacc("TRN2", target_bir_lowering=False, num_devices=1)
    a, f = "L0_attn_", "L0_ffn_"
    vectors = np.concatenate([np.asarray(inputs[a + v]).reshape(-1, P).T for v in (
        "ln_g", "ln_b", "conv_b", "dt_proj_b", "D", "glu_b")], axis=1)
    laid = {
        "x": inputs[a + "x"], "vectors": vectors,
        "in_wT": np.asarray(inputs[a + "in_proj_w"]).T, "conv_w": inputs[a + "conv_w"],
        "x_wT": np.asarray(inputs[a + "x_proj_w"]).T, "dt_wT": np.asarray(inputs[a + "dt_proj_w"]).T,
        "a_log": inputs[a + "A_log"], "out_wT": np.asarray(inputs[a + "out_proj_w"]).T,
        "glu_wT": np.asarray(inputs[a + "glu_w"]).T,
        "router_w": np.concatenate([inputs[f + "gate_w"], inputs[f + "shared_gate_w"]], axis=1),
        "sgu_w": inputs[f + "shared_gate_up_w"], "sdown_w": inputs[f + "shared_down_w"],
        "egu_w": inputs[f + "expert_gate_up_w"], "edown_w": inputs[f + "expert_down_w"],
    }
    arrays, args = {}, []
    for name, v in laid.items():
        v = np.ascontiguousarray(v)
        arrays[name] = v
        args.append(nc.dram_tensor(name, v.shape, mybir.dt.from_np(v.dtype), kind="ExternalInput").ap())
    args.append(nc.dram_tensor("out", [T + CAP, DM], F32, kind="ExternalOutput").ap())
    args.append(nc.dram_tensor("counts", [E, T], F32, kind="Internal").ap())
    args.append(nc.dram_tensor("table", [T, ROW], F32, kind="Internal").ap())
    args.append(nc.dram_tensor("ends", [E * TILES], F32, kind="Internal").ap())
    mamba_moe(nc, *args)
    r = run(nc, [arrays], core_ids=[0])
    return r.results[0]["out"][0:T].reshape(B, L, DM)
```
